# Optimizing a Trainium2 kernel written in Bass

```python
import numpy as np
import jax
import jax.numpy as jnp

def _softmax(x, axis=-1):
    return jax.nn.softmax(x, axis=axis)

def _gelu(x):
    return jax.nn.gelu(x, approximate=True)

def _silu(x):
    return jax.nn.silu(x)

def _sigmoid(x):
    return jax.nn.sigmoid(x)

def _layernorm(x, axis=-1, eps=1e-05):
    m = jnp.mean(x, axis=axis, keepdims=True)
    v = jnp.var(x, axis=axis, keepdims=True)
    return (x - m) / jnp.sqrt(v + eps)

def _scatter_add(tgt, idx, src, axis=0):
    return tgt.at[idx].add(src)

def _segment_sum(src, seg, n):
    return jax.ops.segment_sum(src, seg, n)
kernel_name = 'mk_gnn_resnorm_d2_gnn_r32_783060'

def setup_inputs(seed: int=0):
    np.random.seed(seed)
    _w = jnp.asarray

    def _rec_inputs():
        import jax
        import jax.numpy as jnp
        _gk = jax.random.key(seed)
        x = -0.000202 + 1 * jax.random.normal(jax.random.fold_in(_gk, 1), (3125, 64), jnp.float32)
        _s = jax.random.randint(jax.random.fold_in(_gk, 2), (25000,), 0, 3125, jnp.int32)
        _d = jax.random.randint(jax.random.fold_in(_gk, 3), (25000,), 0, 3125, jnp.int32)
        _loop = jnp.arange(3125, dtype=jnp.int32)
        src = jnp.concatenate([_s, _d, _loop])
        dst = jnp.concatenate([_d, _s, _loop])
        _o = jnp.argsort(dst, stable=True)
        src = src[_o]
        dst = dst[_o]
        edge_attr_64 = -2.25437e-05 + 0.999858 * jax.random.normal(jax.random.fold_in(_gk, 12), (53125, 64), jnp.float32)
        return (x, src, dst, edge_attr_64)
    x, src, dst, edge_attr_64 = _rec_inputs()

    def _L0_gnn_setup():
        import jax, jax.numpy as jnp
        import numpy as np
        N_SRC = 3125
        N_DST = 3125
        N_EDGES = 1250000
        D_IN = 64
        D_OUT = 64
        key = jax.random.key(seed)
        k1, k2, k3, k4 = jax.random.split(key, 4)
        feat = jax.random.normal(k1, (N_SRC, D_IN), dtype=jnp.float32)
        W = jax.random.normal(k2, (D_OUT, D_IN), dtype=jnp.float32) / np.float32(np.sqrt(D_IN))
        src_idx = jax.random.randint(k3, (N_EDGES,), 0, N_SRC, dtype=jnp.int32)
        dst_idx = jax.random.randint(k4, (N_EDGES,), 0, N_DST, dtype=jnp.int32)
        return {'feat': feat, 'W': W, 'src_idx': src_idx, 'dst_idx': dst_idx}
    _L0_gnn_all = _L0_gnn_setup()
    _L0_gnn_in = {k: v for k, v in _L0_gnn_all.items() if k in ('W',)}
    del _L0_gnn_all

    def _L1_gnn_setup():
        import jax, jax.numpy as jnp
        import numpy as np
        N_NODES = 3125
        N_EDGES = 31250
        H = 64
        R = 2
        SCALE = 0.05

        def _gru_cell(x, h, W_ih, W_hh, b_ih, b_hh):
            gx = x @ W_ih + b_ih
            gh = h @ W_hh + b_hh
            xr, xz, xn = jnp.split(gx, 3, axis=1)
            hr, hz, hn = jnp.split(gh, 3, axis=1)
            r = jax.nn.sigmoid(xr + hr)
            z = jax.nn.sigmoid(xz + hz)
            n = jnp.tanh(xn + r * hn)
            return (1.0 - z) * n + z * h
        key = jax.random.key(seed)
        ks = jax.random.split(key, 8)
        h = jax.random.normal(ks[0], (N_NODES, H), jnp.float32)
        e = jax.random.normal(ks[1], (N_EDGES, H), jnp.float32)
        src = jax.random.randint(ks[2], (N_EDGES,), 0, N_NODES, jnp.int32)
        dst = jax.random.randint(ks[3], (N_EDGES,), 0, N_NODES, jnp.int32)
        W_msg = jax.random.normal(ks[4], (R, 3 * H, 2 * H), jnp.float32) * SCALE
        b_msg = jnp.zeros((R, 2 * H), jnp.float32)
        W_ih = jax.random.normal(ks[5], (R, 2 * H, 3 * H), jnp.float32) * SCALE
        W_hh = jax.random.normal(ks[6], (R, H, 3 * H), jnp.float32) * SCALE
        b_ih = jnp.zeros((R, 3 * H), jnp.float32)
        b_hh = jnp.zeros((R, 3 * H), jnp.float32)
        return {'h': h, 'e': e, 'src': src, 'dst': dst, 'W_msg': W_msg, 'b_msg': b_msg, 'W_ih': W_ih, 'W_hh': W_hh, 'b_ih': b_ih, 'b_hh': b_hh}
    _L1_gnn_all = _L1_gnn_setup()
    _L1_gnn_in = {k: v for k, v in _L1_gnn_all.items() if k in ('W_msg', 'b_msg', 'W_ih', 'W_hh', 'b_ih', 'b_hh')}
    del _L1_gnn_all
    return {'x': x, 'src': src, 'dst': dst, 'edge_attr_64': edge_attr_64, 'L0_gnn_W': _L0_gnn_in['W'], 'L1_gnn_W_msg': _L1_gnn_in['W_msg'], 'L1_gnn_b_msg': _L1_gnn_in['b_msg'], 'L1_gnn_W_ih': _L1_gnn_in['W_ih'], 'L1_gnn_W_hh': _L1_gnn_in['W_hh'], 'L1_gnn_b_ih': _L1_gnn_in['b_ih'], 'L1_gnn_b_hh': _L1_gnn_in['b_hh']}

def reference(x, src, dst, edge_attr_64, L0_gnn_W, L1_gnn_W_msg, L1_gnn_b_msg, L1_gnn_W_ih, L1_gnn_W_hh, L1_gnn_b_ih, L1_gnn_b_hh):
    import jax
    import jax.numpy as jnp

    def _L0_gnn_ref(feat, W, src_idx, dst_idx):
        import jax, jax.numpy as jnp
        import numpy as np
        N_SRC = 3125
        N_DST = 3125
        N_EDGES = 1250000
        D_IN = 64
        D_OUT = 64
        h = feat @ W.T
        msg = h[src_idx]
        s = jax.ops.segment_sum(msg, dst_idx, num_segments=N_DST)
        cnt = jax.ops.segment_sum(jnp.ones((msg.shape[0],), feat.dtype), dst_idx, num_segments=N_DST)
        out = jnp.where(cnt[:, None] > 0, s / jnp.maximum(cnt, 1.0)[:, None], 0.0)
        return out

    def _L1_gnn_ref(h, e, src, dst, W_msg, b_msg, W_ih, W_hh, b_ih, b_hh):
        import jax, jax.numpy as jnp
        import numpy as np
        N_NODES = 3125
        N_EDGES = 31250
        H = 64
        R = 2
        SCALE = 0.05

        def _gru_cell(x, h, W_ih, W_hh, b_ih, b_hh):
            gx = x @ W_ih + b_ih
            gh = h @ W_hh + b_hh
            xr, xz, xn = jnp.split(gx, 3, axis=1)
            hr, hz, hn = jnp.split(gh, 3, axis=1)
            r = jax.nn.sigmoid(xr + hr)
            z = jax.nn.sigmoid(xz + hz)
            n = jnp.tanh(xn + r * hn)
            return (1.0 - z) * n + z * h
        N = h.shape[0]
        deg = jax.ops.segment_sum(jnp.ones((dst.shape[0],), h.dtype), dst, num_segments=N)
        has_msg = (deg > 0)[:, None]
        safe_deg = jnp.maximum(deg, 1.0)[:, None]
        act = jnp.zeros((N, 2 * h.shape[1]), h.dtype)
        for t in range(W_msg.shape[0]):
            msg_in = jnp.concatenate([h[dst], h[src], e], axis=1)
            a = msg_in @ W_msg[t] + b_msg[t]
            s = jax.ops.segment_sum(a, dst, num_segments=N)
            act = jnp.where(has_msg, s / safe_deg, act)
            h = _gru_cell(act, h, W_ih[t], W_hh[t], b_ih[t], b_hh[t])
        return h
    x = _layernorm(x + _L0_gnn_ref(x, L0_gnn_W, src, dst), axis=-1)
    x = _layernorm(x + _L1_gnn_ref(x, edge_attr_64, src, dst, L1_gnn_W_msg, L1_gnn_b_msg, L1_gnn_W_ih, L1_gnn_W_hh, L1_gnn_b_ih, L1_gnn_b_hh), axis=-1)
    return x

_drawn_inputs = setup_inputs


def setup_inputs(seed=0):
    import zlib

    import numpy as np

    out = dict(_drawn_inputs(seed))
    spreads = {'L1_gnn_b_msg': (0.0, 0.293), 'L1_gnn_b_ih': (0.0, 0.1), 'L1_gnn_b_hh': (0.0, 0.327)}
    factors = {}
    for name, (base, spread) in spreads.items():
        noise = np.random.default_rng([zlib.crc32(name.encode()), seed]).standard_normal(out[name].shape)
        drawn = base * np.exp(spread * noise) if base else spread * noise
        out[name] = jnp.asarray(drawn.astype(out[name].dtype))
    for name, factor in factors.items():
        out[name] = (out[name] * factor).astype(out[name].dtype)
    return out
```

```python
from contextlib import ExitStack

import concourse.bass as bass
from concourse import mybir

N, H, E = 3125, 64, 53125
P = 125
NB = N // P
EC = E // P
GD, WIN = 5, 128
NG = N // GD
SD, SC = 25, 4
NS = N // SD
SWIN = SC * 128
XMAX2 = float(2 ** 30)
LO = 2048.0
EPS = 1e-5
TILE = 4 * P
NT = 7
UNITS = 3 + (NG + 3) // 4
ITS = 15
KW = 126


def blocks_of(t):
    return range(4 * t, min(4 * t + 4, NB))


class Chain:

    def __init__(self, eng, sem):
        self.eng, self.sem, self.n = eng, sem, 0

    def add(self, ins):
        self.n += 1
        ins.then_inc(self.sem, 1)

    def wait(self):
        self.eng.wait_ge(self.sem, self.n)

    def done(self, ins):
        self.add(ins)
        self.wait()


def build(nc, x, src, dst, e, w0, w_msg, b_msg, w_ih, w_hh, b_ih, b_hh, out):
    f32, f16, bf16, i32 = mybir.dt.float32, mybir.dt.float16, mybir.dt.bfloat16, mybir.dt.int32
    ALU, ACT = mybir.AluOpType, mybir.ActivationFunctionType
    ctx = ExitStack()
    with ctx:
        def sb(name, shape, dt=f32):
            return ctx.enter_context(nc.sbuf_tensor(name, shape, dt))

        def sem(name):
            return ctx.enter_context(nc.semaphore(name))

        big = sb("big", [128, (NB * N + 1) // 2])
        HE = sb("HE", [128, N])
        rdeg = sb("rdeg", [128, N])
        X0 = sb("X0", [128, NB, H])
        work = sb("work", [128, 7400])
        ident = sb("ident", [128, 128])
        onesb = sb("onesb", [128, 128], bf16)
        loscale = sb("loscale", [128, 1])
        eps_col = sb("eps_col", [128, 1])
        w0t = sb("w0t", [128, H])
        w_he = [sb(f"w_he{r}", [128, 4 * H]) for r in range(2)]
        w_ag = [sb(f"w_ag{r}", [128, 3 * H]) for r in range(2)]
        bias3 = [sb(f"bias3{r}", [3, 4 * H], bf16) for r in range(2)]
        flag = sb("flag", [1, 1], i32)
        A3 = big[:, :].bitcast(f16)[:, 0:NB * N].rearrange("p (s d) -> p s d", s=NB)

        def carve(base):
            at = [0]

            def take(n, dt=f32):
                words = n if dt in (f32, i32) else (n + 1) // 2
                piece = base[:, at[0]:at[0] + words]
                at[0] += words
                assert at[0] <= base.shape[1], at[0]
                return piece if dt == f32 else piece.bitcast(dt)[:, 0:n]
            return take

        take = carve(work)
        iota_k = take(128, bf16)
        iota_d = take(SD)
        lo2 = take(2 * NG, bf16).rearrange("p (g t) -> p g t", t=2)
        hi2 = take(2 * NG, bf16).rearrange("p (g t) -> p g t", t=2)
        ecode = take(SC * NS).rearrange("p (s c) -> p s c", c=SC)
        one_lo = [take(10 * 128, bf16).rearrange("p (g k) -> p g k", g=10) for _ in range(2)]
        one_hi = [take(10 * KW, bf16).rearrange("p (g k) -> p g k", g=10) for _ in range(2)]
        one_e = take(8 * SC * SD).rearrange("p (s c d) -> p s c d", s=8, c=SC)
        ering = take(8 * SC * H).rearrange("p (s c f) -> p s c f", s=8, c=SC)
        estart_i = take(NS, i32)
        take = carve(work)
        parts = [take(NB * 2 * H, f16).rearrange("p (b f) -> p b f", b=NB) for _ in range(2)]
        H1 = take(NB * H).rearrange("p (b f) -> p b f", b=NB)
        agg = [take(TILE) for _ in range(2)]
        rz = take(4 * 2 * H).rearrange("p (b f) -> p b f", b=4)
        cand = take(4 * H).rearrange("p (b f) -> p b f", b=4)
        rest = take(4 * H).rearrange("p (b f) -> p b f", b=4)
        bst = take(6 * 4).rearrange("p (b s) -> p b s", b=4)
        mv = take(2 * NB).rearrange("p (b s) -> p b s", b=NB)
        rstd = take(NB)
        take = carve(big)
        dst_i = take(EC + 1, i32)
        src_i = take(EC, i32)
        dst_f, src_f = take(EC + 1), take(EC)
        q5, hi_f, tmp_f, key = take(EC), take(EC), take(EC), take(EC)
        ones = take(128)
        thr = take(6)
        gbase = take(NG)
        sbase = take(NS)
        diag = take(128)
        cnt_row, row_f, ptr_f = take(6), take(6), take(6)
        row_i, ptr_i = take(6, i32), take(6, i32)
        found_i = take(6 * EC, i32).rearrange("p (j c) -> p j c", j=6)
        found_f = take(6 * EC).rearrange("p (j c) -> p j c", j=6)
        kwin = take(5 * WIN).rearrange("p (j c) -> p j c", j=5)
        ewin_i = take(SWIN, i32)
        ewin_f = take(SWIN)
        key_i, lo_i, hi_i = take(NG, i32), take(NG, i32), take(NG, i32)
        hi_c, ok_g = take(NG), take(NG)
        ok_e = take(SC * NS).rearrange("p (s c) -> p s c", c=SC)
        xsq = take(NB * H).rearrange("p (b f) -> p b f", b=NB)
        same, step1 = take(EC), take(EC)
        stats, bad, bad1 = take(5), take(5), take(1)
        w0_in = take(2 * H)
        wm_in = [take(3 * 2 * H).rearrange("p (c k) -> p c k", c=3) for _ in range(2)]
        wi_in = [take(3 * H) for _ in range(2)]
        wh_in = [take(3 * H) for _ in range(2)]
        bm_in = [take(1) for _ in range(2)]
        bi_in, bh_in = [take(3 * H) for _ in range(2)], [take(3 * H) for _ in range(2)]
        wmt = [take(4 * H) for _ in range(2)]
        bm3 = [take(3) for _ in range(2)]
        bias_f = [take(4 * H) for _ in range(2)]
        btmp = take(4 * H)
        bpart = [take(4 * H, bf16) for _ in range(3)]
        bsel = take(4 * H)
        iota_n = take(N)
        one_n = take(N)
        sums = take(N)
        stage = take(2 * H)
        zero_st = take(2 * H)
        idx_now = take(1, i32)
        hneg = take(N)
        w_gen = [take(4 * H) for _ in range(2)]
        wg_l = [take(H + 1) for _ in range(2)]
        maskm1 = take(N)

        PS = ctx.enter_context(nc.psum_tensor("PS", [128, 8, 512], f32))

        def bank(b, cols=512, rows=128, n=1):
            return PS[0:rows, b, 0:cols] if n == 1 else PS[0:rows, b:b + n, 0:cols]

        one_eb = one_e.bitcast(bf16).rearrange("p s c (d t) -> p s c d t", t=2)
        W_LOADS = 16 * (2 + 2 * (4 + 2 * 3))
        key_dram = nc.dram_tensor("key_scratch", [E], f32).ap()
        h_dram = nc.dram_tensor("h_scratch", [N, H], f32).ap()
        out3 = out.rearrange("(b p) f -> p b f", p=P)
        h_dram3 = h_dram.rearrange("(b p) f -> p b f", p=P)

        dst_in, src_in, x_in, w_in = sem("dst_in"), sem("src_in"), sem("x_in"), sem("w_in")
        consts = sem("consts")
        first_diag, first_row = sem("first_diag"), sem("first_row")
        rows_ready, found = sem("rows_ready"), sem("found")
        key_ready, key_out = sem("key_ready"), sem("key_out")
        ptrs_ready, kwin_in, ewin_in = sem("ptrs_ready"), sem("kwin_in"), sem("ewin_in")
        ewin_ready, win_t, est_t = sem("ewin_ready"), sem("win_t"), sem("est_t")
        stats_ready, stats_sum, flag_ready = sem("stats_ready"), sem("stats_sum"), sem("flag_ready")
        wt_ready, wt_copied, wp_ready, w_done = sem("wt_ready"), sem("wt_copied"), sem("wp_ready"), sem("w_done")
        dve_c, act_c, pool_c = sem("dve_c"), sem("act_c"), sem("pool_c")
        one_ready = sem("one_ready")
        onee_ready = sem("onee_ready")
        unit_ready, unit_free = sem("unit_ready"), sem("unit_free")
        esum_ready, esum_free = sem("esum_ready"), sem("esum_free")
        e_in = [sem(f"e_in{i}") for i in range(8)]
        e_used = sem("e_used")
        estart_ready = sem("estart_ready")
        build_c = sem("build_c")
        parts_ready = sem("parts_ready")
        sweep_ready, agg_ready = sem("sweep_ready"), sem("agg_ready")
        gates_ready, gates_free = sem("gates_ready"), sem("gates_free")
        var_ready, std_ready = sem("var_ready"), sem("std_ready")
        rz_ready, cand_ready, tanh_ready = sem("rz_ready"), sem("cand_ready"), sem("tanh_ready")
        h_ready, rest_ready, rest_used = sem("h_ready"), sem("rest_ready"), sem("rest_used")
        ht_ready, he_ready = sem("ht_ready"), sem("he_ready")
        idx_ok, estage_in = sem("idx_ok"), sem("estage_in")
        cand_used, w0t_ready = sem("cand_used"), sem("w0t_ready")
        y_ready, out_done = sem("y_ready"), sem("out_done")
        gen_c, stage_in, gone_ready, gused = sem("gen_c"), sem("stage_in"), sem("gone_ready"), sem("gused")
        pass_zeroed, pass_done, sums_ready = sem("pass_zeroed"), sem("pass_done"), sem("sums_ready")
        gz_ready, hstore, idx_set, neg_ready = sem("gz_ready"), sem("hstore"), sem("idx_set"), sem("neg_ready")

        block = ctx.enter_context(nc.Block())

        @block.sync
        def _(sp):
            sp.dma_start(dst_i[0:P, 0:EC], dst.rearrange("(p c) -> p c", c=EC)).then_inc(dst_in, 16)
            sp.wait_ge(consts, 1)
            sp.dma_start(dst_i[0:P - 1, EC:EC + 1], dst[EC:E].rearrange("(p c) -> p c", c=EC)[:, 0:1],
                         allow_slow_non_contiguous=True).then_inc(dst_in, 16)
            sp.dma_start(src_i[0:P, :], src.rearrange("(p c) -> p c", c=EC)).then_inc(src_in, 16)
            sp.dma_start(X0[0:P, :, :], x.rearrange("(b p) f -> p b f", p=P)).then_inc(x_in, 16)
            sp.wait_ge(key_ready, 1)
            sp.dma_start(key_dram.rearrange("(p c) -> p c", c=EC), key[0:P, :]).then_inc(key_out, 16)

            def load_window(s, slot):
                at = sp.value_load(estart_i[0:1, bass.ds(s, 1)], min_val=0, max_val=E - SWIN)
                sp.dma_start(ering[:, slot, :, :],
                             e[bass.ds(at, SWIN), :].rearrange("(p c) f -> p c f", c=SC)).then_inc(e_in[slot], 16)

            def usual():
                sp.wait_ge(estart_ready, 1)
                for s in range(8):
                    load_window(s, s)
                with sp.Fori(1, ITS) as it:
                    for s in range(8):
                        sp.wait_ge(e_used, it * 8 + (s - 7))
                        load_window(it * 8 + s, s)
                for s in range(5):
                    sp.wait_ge(e_used, ITS * 8 + s - 7)
                    load_window(ITS * 8 + s, s)

            def general():
                sp.wait_ge(gz_ready, 2)
                e3 = e.rearrange("(p c) f -> p c f", c=EC)
                with sp.Fori(0, EC) as c:
                    sp.wait_ge(gused, c + (EC + 1))
                    sp.dma_start(stage[0:P, H:2 * H], e3[:, bass.ds(c, 1), :].rearrange("p c f -> p (c f)")
                                 ).then_inc(estage_in, 16)
                for r, hbuf in ((1, X0), (2, H1)):
                    sp.wait_ge(h_ready, NT * r)
                    sp.dma_start(h_dram3, hbuf[0:P, :, :]).then_inc(hstore, 16)
                    sp.wait_ge(hstore, 16 * r)

            sp.wait_ge(flag_ready, 1)
            bad_inputs = sp.value_load(flag[0:1, 0:1], min_val=0, max_val=5)
            with sp.If(bad_inputs == 0):
                usual()
            with sp.Else():
                general()
            sp.wait_ge(y_ready, 1)
            sp.dma_start(out3, H1[0:P, :, :]).then_inc(out_done, 16)
            sp.wait_ge(out_done, 16)

        @block.gpsimd
        def _(pool):
            pool.memset(dst_i[:, EC:EC + 1], N).then_inc(consts, 1)
            pool.memset(ones, 1.0).then_inc(consts, 1)
            pool.memset(onesb[:, :], 1.0).then_inc(consts, 1)
            pool.memset(ident[:, :], 0.0).then_inc(pool_c, 1)
            pool.wait_ge(pool_c, 1)
            pool.affine_select(out=ident[:, :], in_=ident[:, :], compare_op=ALU.not_equal, fill=1.0, base=0,
                               pattern=[[-1, 128]], channel_multiplier=1).then_inc(consts, 1)
            pool.iota(thr[:, 0:5], pattern=[[GD * P, 5]], base=0, channel_multiplier=GD,
                      allow_small_or_imprecise_dtypes=True).then_inc(consts, 1)
            pool.iota(thr[:, 5:6], pattern=[[0, 1]], base=0, channel_multiplier=SD,
                      allow_small_or_imprecise_dtypes=True).then_inc(consts, 1)
            pool.memset(stats, 0.0).then_inc(consts, 1)
            pool.memset(loscale[0:H, :], 1.0).then_inc(consts, 1)
            pool.wait_ge(consts, 8)
            pool.memset(loscale[H:128, :], 1.0 / LO).then_inc(consts, 1)
            pool.wait_ge(consts, 9)
            pool.memset(eps_col[:, :], EPS).then_inc(consts, 1)
            pool.iota(iota_k, pattern=[[1, 128]], base=0, channel_multiplier=0,
                      allow_small_or_imprecise_dtypes=True).then_inc(consts, 1)
            pool.iota(iota_d, pattern=[[1, SD]], base=0, channel_multiplier=0,
                      allow_small_or_imprecise_dtypes=True).then_inc(consts, 1)
            for j, total in enumerate((E, E, N, E - N, N * H)):
                pool.memset(bad[0:1, j:j + 1], float(total)).then_inc(consts, 1)
            pool.wait_ge(rows_ready, 1)
            dst_rows = dst.rearrange("(r c) -> r c", c=EC)
            for j in range(6):
                pool.indirect_dma_start(out=found_i[0:P, j, :], out_offset=None, in_=dst_rows,
                                        in_offset=bass.IndirectOffsetOnAxis(ap=row_i[0:P, j:j + 1], axis=0)
                                        ).then_inc(found, 16)
            pool.iota(gbase, pattern=[[P, NG]], base=0, channel_multiplier=0,
                      allow_small_or_imprecise_dtypes=True).then_inc(consts, 1)
            pool.iota(sbase, pattern=[[SD, NS]], base=0, channel_multiplier=0,
                      allow_small_or_imprecise_dtypes=True).then_inc(consts, 1)
            pool.wait_ge(ptrs_ready, 1)
            pool.wait_ge(key_out, 16)
            key_rows = key_dram.rearrange("(n o) -> n o", o=1)
            for j in range(5):
                pool.indirect_dma_start(out=kwin[0:P, j, :], out_offset=None, in_=key_rows,
                                        in_offset=bass.IndirectOffsetOnAxis(ap=ptr_i[0:P, j:j + 1], axis=0)
                                        ).then_inc(kwin_in, 16)
            pool.indirect_dma_start(out=ewin_i[0:P, :], out_offset=None, in_=dst.rearrange("(n o) -> n o", o=1),
                                    in_offset=bass.IndirectOffsetOnAxis(ap=ptr_i[0:P, 5:6], axis=0)
                                    ).then_inc(ewin_in, 16)

            def general():
                pool.iota(iota_n, pattern=[[1, N]], base=0, channel_multiplier=0,
                          allow_small_or_imprecise_dtypes=True).then_inc(gz_ready, 1)
                pool.memset(zero_st, 0.0).then_inc(pass_zeroed, 1)
                pool.memset(stage, 1.0).then_inc(pass_zeroed, 1)
                pool.wait_ge(gused, EC + 1)
                pool.memset(stage[:, 0:H], 0.0).then_inc(gz_ready, 1)
                pool.wait_ge(gused, 2 * EC + 1)
                pool.memset(stage[:, H:2 * H], 0.0).then_inc(gz_ready, 1)
                for r in range(3):
                    if r:
                        pool.wait_ge(hstore, 16 * r)
                    table = x if r == 0 else h_dram
                    with pool.Fori(0, EC) as c:
                        pool.wait_ge(gused, c + ((2 + r) * EC + 1))
                        pool.tensor_copy(idx_now[0:P, :], src_i[0:P, bass.ds(c, 1)]).then_inc(idx_set, 1)
                        pool.wait_ge(idx_set, c + (r * EC + 1))
                        pool.sem_inc(idx_ok, 1)
                        pool.indirect_dma_start(out=stage[0:P, 0:H], out_offset=None, in_=table,
                                                in_offset=bass.IndirectOffsetOnAxis(ap=idx_now[0:P, 0:1], axis=0)
                                                ).then_inc(stage_in, 16)

            pool.wait_ge(flag_ready, 1)
            bad_inputs = pool.value_load(flag[0:1, 0:1], min_val=0, max_val=5)
            with pool.If(bad_inputs == 0):
                pool.wait_ge(flag_ready, 1)
            with pool.Else():
                general()

        @block.vector
        def _(dve):
            ch = Chain(dve, dve_c)
            v = nc.vector
            MAGIC = 12582912.0

            dve.wait_ge(dst_in, 32)
            ch.done(v.tensor_copy(dst_f[0:P, :], dst_i[0:P, :]))
            dve.wait_ge(consts, 17)
            v.tensor_scalar(diag[0:P, 0:P], ident[0:P, 0:P], dst_f[0:P, 0:1], None, ALU.mult).then_inc(first_diag, 1)
            ch.done(v.tensor_scalar(q5[0:P, :], dst_f[0:P, 0:EC], 0.2, -0.4, ALU.mult, ALU.add))
            ch.done(v.tensor_scalar(q5[0:P, :], q5[0:P, :], MAGIC, -MAGIC, ALU.add, ALU.add))
            dve.wait_ge(first_row, 1)
            for j in range(6):
                ch.add(v.tensor_scalar(found_f[0:P, j, 0:P], bank(0, P, P), thr[0:P, j:j + 1], None, ALU.is_lt,
                                       ALU.add, accum_out=cnt_row[0:P, j:j + 1]))
            ch.wait()
            ch.done(v.tensor_scalar(row_f[0:P, :], cnt_row[0:P, :], -1.0, 0.0, ALU.add, ALU.max))
            v.tensor_copy(row_i[0:P, :], row_f[0:P, :]).then_inc(rows_ready, 1)
            dve.wait_ge(src_in, 16)
            ch.done(v.tensor_copy(src_f[0:P, :], src_i[0:P, :]))
            ch.done(v.tensor_scalar(hi_f[0:P, :], src_f[0:P, :], 1.0 / P, -(P - 1) / 2.0 / P, ALU.mult, ALU.add))
            ch.done(v.tensor_scalar(hi_f[0:P, :], hi_f[0:P, :], MAGIC, -MAGIC, ALU.add, ALU.add))
            ch.done(v.scalar_tensor_tensor(src_f[0:P, :], hi_f[0:P, :], -float(P), src_f[0:P, :], ALU.mult, ALU.add))
            ch.done(v.scalar_tensor_tensor(tmp_f[0:P, :], hi_f[0:P, :], float(GD), dst_f[0:P, 0:EC], ALU.mult, ALU.add))
            ch.done(v.scalar_tensor_tensor(tmp_f[0:P, :], q5[0:P, :], float(NB * GD - GD), tmp_f[0:P, :], ALU.mult, ALU.add))
            v.scalar_tensor_tensor(key[0:P, :], tmp_f[0:P, :], 128.0, src_f[0:P, :], ALU.mult, ALU.add).then_inc(key_ready, 1)
            dve.wait_ge(found, 6 * 16)
            ch.done(v.tensor_copy(found_f[0:P, :, :], found_i[0:P, :, :]))
            for j in range(6):
                ch.add(v.tensor_scalar(found_f[0:P, j, :], found_f[0:P, j, :], thr[0:P, j:j + 1], None, ALU.is_lt,
                                       ALU.add, accum_out=cnt_row[0:P, j:j + 1]))
            ch.wait()
            ch.done(v.scalar_tensor_tensor(ptr_f[0:P, :], row_f[0:P, :], float(EC), cnt_row[0:P, :], ALU.mult, ALU.add))
            ch.done(v.tensor_scalar(ptr_f[0:P, 0:5], ptr_f[0:P, 0:5], float(E - WIN), None, ALU.min))
            ch.done(v.tensor_scalar(ptr_f[0:P, 5:6], ptr_f[0:P, 5:6], float(E - SWIN), None, ALU.min))
            v.tensor_copy(ptr_i[0:P, :], ptr_f[0:P, :]).then_inc(ptrs_ready, 1)

            ch.done(v.tensor_tensor(same[0:P, :], dst_f[0:P, 1:EC + 1], dst_f[0:P, 0:EC], ALU.subtract))
            ch.done(v.tensor_scalar(step1[0:P, :], same[0:P, :], 1.0, None, ALU.is_equal, ALU.add,
                                    accum_out=stats[0:P, 2:3]))
            ch.done(v.tensor_scalar(step1[0:P, :], same[0:P, :], 0.0, None, ALU.is_equal, ALU.add,
                                    accum_out=stats[0:P, 3:4]))
            dve.wait_ge(x_in, 16)
            ch.done(v.tensor_tensor(xsq[0:P, :, :], X0[0:P, :, :], X0[0:P, :, :], ALU.mult))
            ch.done(v.tensor_scalar(xsq[0:P, :, :], xsq[0:P, :, :], XMAX2, None, ALU.is_le, ALU.add,
                                    accum_out=stats[0:P, 4:5]))
            dve.wait_ge(est_t, 1)
            v.tensor_copy(estart_i[0:1, :], bank(3, NS, 1)).then_inc(estart_ready, 1)
            dve.wait_ge(ewin_in, 16)
            v.tensor_copy(ewin_f[0:P, :], ewin_i[0:P, :]).then_inc(ewin_ready, 1)

            dve.wait_ge(win_t, 1)
            ch.done(v.tensor_copy(key_i[:, 0:500], bank(0, 500)))
            ch.done(v.tensor_copy(key_i[:, 500:NG], bank(1, NG - 500)))
            dve.wait_ge(consts, 19)
            ch.done(v.tensor_scalar(lo_i, key_i, 127, None, ALU.bitwise_and))
            ch.done(v.tensor_scalar(hi_i, key_i, 7, None, ALU.logical_shift_right))
            v.tensor_copy(lo2, lo_i.unsqueeze(2).to_broadcast([128, NG, 2]))
            ch.done(v.tensor_tensor(hi_c, hi_i, gbase, ALU.subtract))
            v.tensor_copy(hi2, hi_c.unsqueeze(2).to_broadcast([128, NG, 2]))
            ch.done(v.tensor_scalar(ok_g, hi_c, 0.0, None, ALU.is_ge))
            ch.done(v.scalar_tensor_tensor(hi_c, hi_c, float(NB * GD), ok_g, ALU.is_lt, ALU.mult,
                                           accum_out=stats[:, 0:1]))
            dve.wait_ge(win_t, 2)
            ch.done(v.tensor_tensor(ecode, bank(2, SC * NS).rearrange("p (c s) -> p s c", c=SC),
                                    sbase.unsqueeze(2).to_broadcast([128, NS, SC]), ALU.subtract))
            ch.done(v.tensor_scalar(ok_e, ecode, 0.0, None, ALU.is_ge))
            ch.done(v.scalar_tensor_tensor(ok_e, ecode, float(SD), ok_e, ALU.is_lt, ALU.mult,
                                           accum_out=stats[:, 1:2]))
            dve.sem_inc(stats_ready, 1)
            dve.wait_ge(stats_sum, 1)
            ch.done(v.tensor_tensor(bad[0:1, :], bank(3, 5, 1), bad[0:1, :], ALU.not_equal))
            ch.done(v.tensor_reduce(bad1[0:1, :], bad[0:1, :], mybir.AxisListType.X, ALU.add))
            v.tensor_copy(flag[0:1, :], bad1[0:1, :]).then_inc(flag_ready, 1)

            for r in range(2):
                dve.wait_ge(wp_ready, r + 1)
                prod, prod_ag = bank(4, 3 * H), bank(7, 3 * H)
                ch.done(v.tensor_tensor(w_he[r][0:H, 0:2 * H], prod[0:H, 0:2 * H], wh_in[r][0:H, 0:2 * H], ALU.add))
                ch.done(v.tensor_copy(w_he[r][0:H, 2 * H:3 * H], prod[0:H, 2 * H:3 * H]))
                ch.done(v.tensor_copy(w_he[r][0:H, 3 * H:4 * H], wh_in[r][0:H, 2 * H:3 * H]))
                ch.done(v.tensor_copy(w_he[r][H:128, 0:3 * H], prod[H:128, 0:3 * H]))
                ch.done(v.memset(w_he[r][H:128, 3 * H:4 * H], 0.0))
                ch.done(v.tensor_scalar(w_ag[r][:, :], prod_ag, loscale[:, 0:1], None, ALU.mult))
                bf = bias_f[r][0:3, :]
                ch.done(v.tensor_tensor(bf[:, 0:3 * H], bank(5, 3 * H, 3), bi_in[r][0:3, :], ALU.add))
                ch.done(v.tensor_tensor(bf[:, 0:2 * H], bf[:, 0:2 * H], bh_in[r][0:3, 0:2 * H], ALU.add))
                ch.done(v.tensor_copy(bf[:, 3 * H:4 * H], bh_in[r][0:3, 2 * H:3 * H]))
                for k in range(3):
                    ch.done(v.tensor_copy(bpart[k][0:3, :], bf))
                    if k < 2:
                        ch.done(v.tensor_tensor(bf, bf, bpart[k][0:3, :], ALU.subtract))
                ch.done(v.tensor_scalar(bsel[0:3, :], bpart[0][0:3, :], ident[0:3, 0:1], None, ALU.mult))
                ch.done(v.scalar_tensor_tensor(bsel[0:3, :], bpart[1][0:3, :], ident[0:3, 1:2], bsel[0:3, :], ALU.mult, ALU.add))
                ch.done(v.scalar_tensor_tensor(bsel[0:3, :], bpart[2][0:3, :], ident[0:3, 2:3], bsel[0:3, :], ALU.mult, ALU.add))
                v.tensor_copy(bias3[r][0:3, :], bsel[0:3, :]).then_inc(w_done, 1)
            dve.wait_ge(w0t_ready, 1)
            v.tensor_scalar(w0t[:, :], bank(6, H), loscale[:, 0:1], None, ALU.mult).then_inc(w_done, 1)

            def build_step(it, ng, ns):
                dve.wait_ge(esum_ready, it + 1)
                for k in range(0, ns, 4):
                    m = min(4, ns - k)
                    v.tensor_tensor(one_e[:, k:k + m, :, :],
                                    ecode[:, bass.ds(it * 8 + k, m), :].unsqueeze(3).to_broadcast([128, m, SC, SD]),
                                    iota_d.unsqueeze(1).unsqueeze(1).to_broadcast([128, m, SC, SD]),
                                    ALU.is_equal).then_inc(onee_ready, 1)
                for h in range((ng + 9) // 10):
                    m = min(10, ng - 10 * h)
                    dve.wait_ge(unit_ready, it * 10 + (1, 3, 6, 8)[h])
                    for two, codes, w in ((one_lo[h % 2], lo2, 128), (one_hi[h % 2], hi2, KW)):
                        v.tensor_tensor(
                            two[:, 0:m, :].rearrange("p g (k t) -> p g k t", t=2),
                            codes[:, bass.ds(it * 40 + 10 * h, m), :].unsqueeze(2).to_broadcast([128, m, w // 2, 2]),
                            iota_k[:, 0:w].rearrange("p (k t) -> p k t", t=2).unsqueeze(1).to_broadcast([128, m, w // 2, 2]),
                            ALU.is_equal).then_inc(one_ready, 1)
                cols = bass.ds(it * 200, ns * SD)
                dve.wait_ge(esum_ready, it + 2)
                v.reciprocal(rdeg[:, cols], bank(6, ns * SD)).then_inc(build_c, 1)
                dve.wait_ge(build_c, it + 1)
                v.tensor_tensor(HE[H:128, cols], PS[H:128, 5, 0:ns * SD], rdeg[H:128, cols], ALU.mult
                                ).then_inc(esum_free, 1)

            def mean(T, t, gen):
                w = len(blocks_of(t)) * P
                if T >= 2:
                    dve.wait_ge(gates_ready, T - 1)
                if gen:
                    from_ = sums[:, TILE * t:TILE * t + w]
                else:
                    dve.wait_ge(sweep_ready, T + 1)
                    from_ = bank(T % 2, w)
                v.tensor_tensor(agg[T % 2][:, 0:w], from_, rdeg[:, TILE * t:TILE * t + w], ALU.mult
                                ).then_inc(agg_ready, 1)

            def moments(y, t):
                for i, b in enumerate(blocks_of(t)):
                    ch.add(v.bn_stats(bst[0:P, i, :], y[0:P, b, :]))
                ch.wait()
                for i, b in enumerate(blocks_of(t)):
                    ch.add(v.bn_aggr(mv[0:P, b, :], bst[0:P, i, :]))
                ch.wait()

            def normalize(y, blks):
                for b in blks:
                    ch.add(v.tensor_scalar(y[0:P, b, :], y[0:P, b, :], mv[0:P, b, 0:1], rstd[0:P, b:b + 1],
                                           ALU.subtract, ALU.mult))
                ch.wait()

            def hand_over(T, h, t, gen):
                blks = blocks_of(t)
                sl = slice(blks[0], blks[-1] + 1)
                if gen:
                    dve.sem_inc(h_ready, 1)
                    return
                p = parts[(T // NT + 1) % 2]
                v.tensor_copy(p[0:P, sl, 0:H], h[0:P, sl, :]).then_inc(h_ready, 1)
                dve.wait_ge(h_ready, T + 1)
                if T >= 1:
                    dve.wait_ge(rest_used, T)
                v.tensor_tensor(rest[0:P, 0:len(blks), :], h[0:P, sl, :], p[0:P, sl, 0:H], ALU.subtract
                                ).then_inc(rest_ready, 1)

            def gcn(t, gen):
                T, blks = t, blocks_of(t)
                n, sl = len(blks), slice(blks[0], blks[-1] + 1)
                mean(T, t, gen)
                dve.wait_ge(gates_ready, T + 1)
                ins = v.tensor_tensor(X0[0:P, sl, :], X0[0:P, sl, :],
                                      bank(2 + 2 * (T % 2), n * H, P).rearrange("p (b f) -> p b f", f=H), ALU.add)
                ins.then_inc(gates_free, 1)
                dve.wait_ge(gates_free, T + 1)
                moments(X0, t)
                v.tensor_copy(rstd[0:P, sl], mv[0:P, sl, 1]).then_inc(var_ready, 1)
                dve.wait_ge(std_ready, T + 1)
                ch.done(v.reciprocal(rstd[0:P, sl], rstd[0:P, sl]))
                normalize(X0, blks)
                hand_over(T, X0, t, gen)

            def gru(r, t, gen):
                T, blks = NT * (r + 1) + t, blocks_of(t)
                n, sl = len(blks), slice(blks[0], blks[-1] + 1)
                old = X0 if r == 0 else H1
                gates = bank(2 + 2 * (T % 2), 512, P, 2).rearrange("p a (b f) -> p (a b) f", b=2)
                mean(T, t, gen)
                dve.wait_ge(rz_ready, T - NT + 1)
                ch.done(v.tensor_tensor(cand[0:P, 0:n, :], rz[0:P, 0:n, 0:H], gates[:, 0:n, 3 * H:4 * H], ALU.mult))
                v.tensor_tensor(cand[0:P, 0:n, :], cand[0:P, 0:n, :], gates[:, 0:n, 2 * H:3 * H], ALU.add
                                ).then_inc(gates_free, 1)
                dve.wait_ge(tanh_ready, T - NT + 1)
                ch.done(v.tensor_tensor(H1[0:P, sl, :], old[0:P, sl, :], cand[0:P, 0:n, :], ALU.subtract))
                ch.done(v.tensor_tensor(H1[0:P, sl, :], H1[0:P, sl, :], rz[0:P, 0:n, H:2 * H], ALU.mult))
                v.tensor_tensor(H1[0:P, sl, :], H1[0:P, sl, :], cand[0:P, 0:n, :], ALU.add).then_inc(cand_used, 1)
                dve.wait_ge(cand_used, T - NT + 1)
                if r == 0:
                    hand_over(T, H1, t, gen)
                else:
                    ch.done(v.tensor_tensor(H1[0:P, sl, :], H1[0:P, sl, :], X0[0:P, sl, :], ALU.add))
                    moments(H1, t)

            def rounds(gen):
                for t in range(NT):
                    gcn(t, gen)
                for r in range(2):
                    if gen:
                        neg_h(r)
                        general_pass(3 + r)
                    for t in range(NT):
                        gru(r, t, gen)
                v.tensor_copy(rstd[0:P, :], mv[0:P, :, 1]).then_inc(var_ready, 1)
                dve.wait_ge(std_ready, NT + 1)
                ch.done(v.reciprocal(rstd[0:P, :], rstd[0:P, :]))
                normalize(H1, range(NB))
                dve.sem_inc(y_ready, 1)

            def usual():
                dve.sem_inc(esum_free, 1)
                with dve.Fori(0, ITS) as it:
                    build_step(it, 40, 8)
                build_step(ITS, 25, 5)
                dve.wait_ge(unit_ready, UNITS)
                ch.done(v.tensor_copy(parts[0][0:P, :, 0:H], X0[0:P, :, :]))
                ch.done(v.tensor_tensor(H1[0:P, :, :], X0[0:P, :, :], parts[0][0:P, :, 0:H], ALU.subtract))
                v.tensor_scalar(parts[0][0:P, :, H:2 * H], H1[0:P, :, :], LO, None, ALU.mult).then_inc(parts_ready, 1)
                rounds(False)

            def general_pass(q):
                with dve.Fori(0, EC) as c:
                    dve.wait_ge(gused, c + (q * EC + 1))
                    v.tensor_scalar(one_n[0:P, :], iota_n[0:P, :], dst_f[0:P, bass.ds(c, 1)], None, ALU.is_equal
                                    ).then_inc(gone_ready, 1)
                dve.wait_ge(pass_done, q + 1)
                for t in range(NT):
                    w = len(blocks_of(t)) * P
                    ch.add(v.tensor_copy(sums[:, TILE * t:TILE * t + w], bank(t, w)))
                ch.wait()
                dve.sem_inc(sums_ready, 1)

            def neg_h(r):
                dve.wait_ge(he_ready, NT * (r + 1))
                ch.done(v.tensor_tensor(hneg[0:H, :], maskm1[0:H, :], HE[0:H, :], ALU.mult))
                v.tensor_copy(hneg[H:H + 1, :], maskm1[H:H + 1, :]).then_inc(neg_ready, 1)

            def general():
                dve.wait_ge(gz_ready, 1)
                for r in range(2):
                    ch.done(v.tensor_copy(wg_l[r][:, 0:H], wmt[r][:, 0:H]))
                    v.tensor_copy(wg_l[r][:, H:H + 1], bm_in[r]).then_inc(gen_c, 1)
                for r in range(2):
                    dve.wait_ge(gen_c, 3 + r)
                    ch.done(v.tensor_copy(w_gen[r][0:H + 1, 0:3 * H], bank(r, 3 * H, H + 1)))
                    v.memset(w_gen[r][0:H + 1, 3 * H:4 * H], 0.0).then_inc(neg_ready, 1)
                general_pass(0)
                ch.done(v.tensor_scalar(maskm1, sums, 1.0, -1.0, ALU.min, ALU.add))
                ch.done(v.tensor_scalar(sums, sums, 1.0, None, ALU.max))
                ch.done(v.reciprocal(rdeg[:, :], sums))
                general_pass(1)
                ch.done(v.tensor_tensor(HE[H:128, :], sums[H:128, :], rdeg[H:128, :], ALU.mult))
                general_pass(2)
                rounds(True)

            dve.wait_ge(flag_ready, 1)
            bad_inputs = dve.value_load(flag[0:1, 0:1], min_val=0, max_val=5)
            base = ch.n
            with dve.If(bad_inputs == 0):
                usual()
            ch.n = base
            with dve.Else():
                general()

        @block.scalar
        def _(act):
            a = nc.scalar
            for half in range(2):
                act.dma_start(w0_in[0:H, half * H:(half + 1) * H], w0).then_inc(w_in, 16)
            for r in range(2):
                act.dma_start(wm_in[r][0:H, :, :], w_msg[r].rearrange("(c p) k -> p c k", p=H)).then_inc(w_in, 16)
                act.dma_start(wi_in[r], w_ih[r]).then_inc(w_in, 16)
                act.dma_start(wh_in[r][0:H, :], w_hh[r]).then_inc(w_in, 16)
                act.dma_start(bm_in[r], b_msg[r].rearrange("(k o) -> k o", o=1)).then_inc(w_in, 16)
                for k in range(3):
                    act.dma_start(bi_in[r][k:k + 1, :], b_ih[r:r + 1, :]).then_inc(w_in, 16)
                    act.dma_start(bh_in[r][k:k + 1, :], b_hh[r:r + 1, :]).then_inc(w_in, 16)
            act.wait_ge(w_in, W_LOADS)
            for r in range(2):
                act.activation(bm3[r], bm_in[r].to_broadcast([128, 3]), ACT.Copy).then_inc(act_c, 1)
                act.wait_ge(wt_ready, r + 1)
                act.activation(wmt[r], bank(6 + r, 4 * H), ACT.Copy).then_inc(wt_copied, 1)

            def unit(it, u, n):
                act.wait_ge(unit_ready, it * 10 + (u + 4))
                act.activation(
                    A3[:, :, bass.ds(it * 200 + 20 * u, n * GD)].rearrange("p s (g d) -> p s g d", g=n),
                    bank(u % 5, n * P).rearrange("p (g s d) -> p s g d", g=n, d=GD), ACT.Copy
                ).then_inc(unit_free, 1)

            def rounds(gen):
                def hand_over(T, t):
                    blks = blocks_of(t)
                    n, w, sl = len(blks), len(blks) * P, slice(blks[0], blks[-1] + 1)
                    if not gen:
                        act.wait_ge(rest_ready, T + 1)
                        a.activation(parts[(T // NT + 1) % 2][0:P, sl, H:2 * H], rest[0:P, 0:n, :], ACT.Copy,
                                     scale=LO).then_inc(rest_used, 1)
                    act.wait_ge(ht_ready, T + 1)
                    a.activation(HE[0:H, TILE * t:TILE * t + w], bank(6, w, H), ACT.Copy).then_inc(he_ready, 1)

                for t in range(NT):
                    blks = blocks_of(t)
                    sl = slice(blks[0], blks[-1] + 1)
                    act.wait_ge(var_ready, t + 1)
                    a.activation(rstd[0:P, sl], rstd[0:P, sl], ACT.Sqrt, bias=eps_col[0:P, 0:1]).then_inc(std_ready, 1)
                    hand_over(t, t)
                for r in range(2):
                    for t in range(NT):
                        T, n = NT * (r + 1) + t, len(blocks_of(t))
                        gates = bank(2 + 2 * (T % 2), 512, P, 2).rearrange("p a (b f) -> p (a b) f", b=2)
                        act.wait_ge(gates_ready, T + 1)
                        if T > NT:
                            act.wait_ge(cand_used, T - NT)
                        a.activation(rz[0:P, 0:n, :], gates[:, 0:n, 0:2 * H], ACT.Sigmoid).then_inc(rz_ready, 1)
                        act.wait_ge(gates_free, T + 1)
                        a.activation(cand[0:P, 0:n, :], cand[0:P, 0:n, :], ACT.Tanh).then_inc(tanh_ready, 1)
                        if r == 0:
                            hand_over(T, t)
                act.wait_ge(var_ready, NT + 1)
                a.activation(rstd[0:P, :], rstd[0:P, :], ACT.Sqrt, bias=eps_col[0:P, 0:1]).then_inc(std_ready, 1)

            def usual():
                act.sem_inc(unit_free, 5)
                with act.Fori(0, ITS) as it:
                    for u in range(10):
                        unit(it, u, 4)
                for u in range(7):
                    unit(ITS, u, 4 if u < 6 else 1)
                rounds(False)

            act.wait_ge(flag_ready, 1)
            bad_inputs = act.value_load(flag[0:1, 0:1], min_val=0, max_val=5)
            with act.If(bad_inputs == 0):
                usual()
            with act.Else():
                rounds(True)

        @block.tensor
        def _(pe):
            mm = nc.tensor.matmul

            pe.wait_ge(first_diag, 1)
            mm(bank(0, P, P), ones[0:P, 0:P], diag[0:P, 0:P], start=True, stop=True).then_inc(first_row, 1)
            pe.wait_ge(w_in, W_LOADS)
            for r in range(2):
                for k, c in enumerate((0, 2, 1, 1)):
                    ins = nc.tensor.transpose(bank(6 + r, 4 * H)[:, k * H:(k + 1) * H], wm_in[r][0:H, c, :],
                                              ident[0:H, 0:H])
                ins.then_inc(wt_ready, 1)
            pe.wait_ge(ptrs_ready, 1)
            mm(bank(3, NS, 1), ptr_f[0:P, 5:6], ident[0:P, 0:P], start=True, stop=True).then_inc(est_t, 1)
            pe.wait_ge(kwin_in, 5 * 16)
            for j in range(5):
                ins = nc.tensor.transpose(bank(j // 4)[:, (j % 4) * P:(j % 4) * P + P], kwin[0:P, j, :], ident[0:P, 0:P])
            ins.then_inc(win_t, 1)
            pe.wait_ge(ewin_ready, 1)
            for c in range(SC):
                ins = nc.tensor.transpose(bank(2)[:, c * NS:(c + 1) * NS],
                                          ewin_f[0:P, :].rearrange("p (e c) -> p e c", c=SC)[:, :, c], ident[0:P, 0:P])
            ins.then_inc(win_t, 1)
            pe.wait_ge(stats_ready, 1)
            mm(bank(3, 5, 1), ones[:, 0:1], stats, start=True, stop=True).then_inc(stats_sum, 1)

            pe.wait_ge(wt_copied, 2)
            for r in range(2):
                if r:
                    pe.wait_ge(w_done, 1)
                mm(bank(4)[:, 0:3 * H], wmt[r][:, 0:2 * H], wi_in[r], start=True, stop=True)
                mm(bank(7)[:, 0:3 * H], wmt[r][:, 2 * H:4 * H], wi_in[r], start=True, stop=True)
                mm(bank(5, 3 * H, 3), bm3[r], wi_in[r], start=True, stop=True).then_inc(wp_ready, 1)
            nc.tensor.transpose(bank(6, H), w0_in[0:H, :], ident[0:H, 0:H]).then_inc(w0t_ready, 1)

            def build_step(it, ng, ns):
                def adjacency(h):
                    m = min(10, ng - 10 * h)
                    pe.wait_ge(one_ready, it * 8 + (2 * h + 2))
                    for i in range(m):
                        g = 10 * h + i
                        u, k = g // 4, g % 4
                        if k == 0:
                            pe.wait_ge(unit_free, it * 10 + (u + 1))
                        ins = mm(bank(u % 5)[:, k * P:k * P + P], one_lo[h % 2][:, i, :], one_hi[h % 2][:, i, 0:P],
                                 start=True, stop=True)
                        if k == 3 or g == ng - 1:
                            ins.then_inc(unit_ready, 1)

                def edge_features(k):
                    m = min(4, ns - k)
                    pe.wait_ge(onee_ready, it * 2 + (k // 4 + 1))
                    for s in range(k, k + m):
                        pe.wait_ge(e_in[s], it * 16 + 16)
                        for c in range(SC):
                            ins = mm(PS[H:128, 5, s * SD:(s + 1) * SD], ering[:, s, c, :], one_e[:, s, c, :],
                                     start=(c == 0), stop=(c == SC - 1))
                        ins.then_inc(e_used, 1)

                halves = (ng + 9) // 10
                pe.wait_ge(esum_free, it + 1)
                adjacency(0)
                edge_features(0)
                adjacency(1)
                edge_features(4)
                for c in range(SC):
                    ins = mm(bank(6, ns * SD).rearrange("p (s d) -> p s d", d=SD), onesb[:, :],
                             one_eb[:, 0:ns, c, :, 1], start=(c == 0), stop=(c == SC - 1))
                ins.then_inc(esum_ready, 1)
                for h in range(2, halves):
                    adjacency(h)

            def sweep(T, t):
                w = len(blocks_of(t)) * P
                if t == 0:
                    if T == 0:
                        pe.wait_ge(parts_ready, 1)
                    else:
                        pe.wait_ge(h_ready, T)
                        pe.wait_ge(rest_used, T)
                if T >= 2:
                    pe.wait_ge(agg_ready, T - 1)
                p = parts[(T // NT) % 2]
                for s in range(NB):
                    ins = mm(bank(T % 2, w), p[0:P, s, :], A3[0:P, s, TILE * t:TILE * t + w],
                             start=(s == 0), stop=(s == NB - 1))
                ins.then_inc(sweep_ready, 1)

            def dense(T, t, gen):
                if T >= 2:
                    pe.wait_ge(gates_free, T - 1)
                pe.wait_ge(agg_ready, T + 1)
                r = T // NT - 1
                for i, b in enumerate(blocks_of(t)):
                    mean = agg[T % 2][:, i * P:(i + 1) * P]
                    own = HE[:, b * P:(b + 1) * P]
                    if r < 0:
                        ins = mm(PS[0:P, 2 + 2 * (T % 2), i * H:(i + 1) * H], mean, w0t[:, :], start=True, stop=True)
                        continue
                    at = 2 + 2 * (T % 2) + i // 2
                    lo = (i % 2) * 4 * H
                    mm(PS[0:P, at, lo:lo + 4 * H], own, w_he[r][:, :], start=True, stop=False)
                    mm(PS[0:P, at, lo:lo + 3 * H], mean, w_ag[r][:, :], start=False, stop=False)
                    if gen:
                        mm(PS[0:P, at, lo:lo + 4 * H], hneg[0:H + 1, b * P:(b + 1) * P], w_gen[r][0:H + 1, :],
                           start=False, stop=False)
                    ins = mm(PS[0:P, at, lo:lo + 4 * H], onesb[0:3, 0:P], bias3[r][0:3, :], start=False, stop=True)
                ins.then_inc(gates_ready, 1)

            def transposed(T, t, h):
                pe.wait_ge(h_ready, T + 1)
                if T >= 1:
                    pe.wait_ge(he_ready, T)
                for i, b in enumerate(blocks_of(t)):
                    ins = nc.tensor.transpose(bank(6, 512, H)[:, i * P:(i + 1) * P], h[0:P, b, :], ident[0:P, 0:P])
                ins.then_inc(ht_ready, 1)

            def rounds(gen):
                for rnd in range(3):
                    if gen:
                        general_pass(2 + rnd)
                    h = (X0, H1, None)[rnd]
                    if rnd:
                        pe.wait_ge(he_ready, NT * rnd)
                    if not gen:
                        sweep(NT * rnd, 0)
                    for t in range(NT):
                        T = NT * rnd + t
                        if not gen and t + 1 < NT:
                            sweep(T + 1, t + 1)
                        dense(T, t, gen)
                        if t and h is not None:
                            transposed(T - 1, t - 1, h)
                    if h is not None:
                        transposed(NT * rnd + NT - 1, NT - 1, h)

            def usual():
                pe.sem_inc(unit_ready, 3)
                pe.sem_inc(esum_ready, 1)
                with pe.Fori(0, ITS) as it:
                    build_step(it, 40, 8)
                build_step(ITS, 25, 5)
                pe.wait_ge(unit_free, 5 + UNITS - 3)
                pe.wait_ge(esum_free, ITS + 2)
                rounds(False)

            def general_pass(q):
                if q:
                    pe.wait_ge(sums_ready, q)
                if q > 2:
                    pe.wait_ge(he_ready, NT * (q - 2))
                    pe.wait_ge(gates_free, NT * (q - 2))
                    pe.wait_ge(neg_ready, 2 + q - 2)
                if q == 0:
                    pe.wait_ge(pass_zeroed, 2)
                tiles = [(t, len(blocks_of(t)) * P) for t in range(NT)]
                for t, w in tiles:
                    mm(bank(t, w), zero_st[0:P, :], iota_n[0:P, TILE * t:TILE * t + w], start=True, stop=False)
                with pe.Fori(0, EC) as c:
                    pe.wait_ge(gone_ready, c + (q * EC + 1))
                    if q == 1:
                        pe.wait_ge(estage_in, c * 16 + 16)
                    if q >= 2:
                        pe.wait_ge(stage_in, c * 16 + ((q - 2) * EC + 1) * 16)
                    for t, w in tiles:
                        ins = mm(bank(t, w), stage[0:P, :], one_n[0:P, TILE * t:TILE * t + w], start=False, stop=False)
                    ins.then_inc(gused, 1)
                for t, w in tiles:
                    ins = mm(bank(t, w), zero_st[0:P, :], iota_n[0:P, TILE * t:TILE * t + w], start=False, stop=True)
                ins.then_inc(pass_done, 1)

            def general():
                pe.wait_ge(gen_c, 2)
                for r in range(2):
                    mm(bank(r, 3 * H, H + 1), wg_l[r], wi_in[r], start=True, stop=True).then_inc(gen_c, 1)
                pe.wait_ge(neg_ready, 2)
                pe.wait_ge(gz_ready, 1)
                pe.sem_inc(gused, 1)
                general_pass(0)
                general_pass(1)
                rounds(True)

            pe.wait_ge(w_done, 3)
            pe.wait_ge(flag_ready, 1)
            bad_inputs = pe.value_load(flag[0:1, 0:1], min_val=0, max_val=5)
            with pe.If(bad_inputs == 0):
                usual()
            with pe.Else():
                general()


_INS = ["x", "src", "dst", "edge_attr_64", "L0_gnn_W", "L1_gnn_W_msg", "L1_gnn_b_msg", "L1_gnn_W_ih", "L1_gnn_W_hh",
        "L1_gnn_b_ih", "L1_gnn_b_hh"]


def kernel(**inputs):
    import numpy as np
    import concourse.bacc as bacc
    from concourse.bass_utils import run_bass_kernel_spmd

    nc = bacc.Bacc("TRN2", target_bir_lowering=False, num_devices=1, dynamic_dma_scratch_size=4096)
    arrays, args = {}, []
    for name in _INS:
        a = np.ascontiguousarray(inputs[name])
        arrays[f"in_{name}"] = a
        args.append(nc.dram_tensor(f"in_{name}", a.shape, mybir.dt.from_np(a.dtype), kind="ExternalInput").ap())
    out = nc.dram_tensor("out_0", (N, H), mybir.dt.float32, kind="ExternalOutput").ap()
    build(nc, *args, out)
    r = run_bass_kernel_spmd(nc, [arrays], core_ids=[0])
    return r.results[0]["out_0"]
```

```python
from contextlib import ExitStack

import concourse.bass as bass
from concourse import mybir

N, H, E = 3125, 64, 53125
P = 125
NB = N // P
EC = E // P
GD, WIN = 5, 128
NG = N // GD
SD, SC = 25, 4
NS = N // SD
SWIN = SC * 128
XMAX2 = float(2 ** 30)
LO = 2048.0
EPS = 1e-5
TILE = 4 * P
NT = 7
STEP = 2 * P
ITS = N // STEP
SG, SS, SU = STEP // GD, STEP // SD, 13
LG, LS, LU = SG // 2, SS // 2, 7
BATCHES = tuple((8 * i, 8 if i < 5 else 10) for i in range(6))
UCREDIT = 6
UBANK = (0, 1, 2, 3, 6)
KW = 126


def blocks_of(t):
    return range(4 * t, min(4 * t + 4, NB))


class Chain:

    def __init__(self, eng, sem, base=0):
        self.eng, self.sem, self.n, self.base = eng, sem, 0, base

    def add(self, ins):
        self.n += 1
        ins.then_inc(self.sem, 1)

    def wait(self):
        self.eng.wait_ge(self.sem, self.base + self.n)

    def done(self, ins):
        self.add(ins)
        self.wait()


def build(nc, x, src, dst, e, w0, w_msg, b_msg, w_ih, w_hh, b_ih, b_hh, out):
    f32, f16, bf16, i32 = mybir.dt.float32, mybir.dt.float16, mybir.dt.bfloat16, mybir.dt.int32
    ALU, ACT = mybir.AluOpType, mybir.ActivationFunctionType
    ctx = ExitStack()
    with ctx:
        def sb(name, shape, dt=f32):
            return ctx.enter_context(nc.sbuf_tensor(name, shape, dt))

        def sem(name):
            return ctx.enter_context(nc.semaphore(name))

        big = sb("big", [128, (NB * N + 1) // 2])
        HE = sb("HE", [128, N])
        rdeg = sb("rdeg", [128, N])
        mv = sb("mv", [128, NB, 2])
        rstd = sb("rstd", [128, NB])
        rnode = sb("rnode", [128, NB])
        X0 = sb("X0", [128, NB, H])
        work = sb("work", [128, 7630])
        ident = sb("ident", [128, 128])
        ones = sb("ones", [128, 128])
        onesb = sb("onesb", [128, 128], bf16)
        loscale = sb("loscale", [128, 1])
        eps_col = sb("eps_col", [128, 1])
        w0t = sb("w0t", [128, H])
        w_he = [sb(f"w_he{r}", [128, 4 * H]) for r in range(2)]
        w_ag = [sb(f"w_ag{r}", [128, 3 * H]) for r in range(2)]
        bias3 = [sb(f"bias3{r}", [3, 4 * H], bf16) for r in range(2)]
        flag = sb("flag", [1, 1], i32)
        A3 = big[:, :].bitcast(f16)[:, 0:NB * N].rearrange("p (s d) -> p s d", s=NB)

        def carve(base):
            at = [0]

            def take(n, dt=f32):
                words = n if dt in (f32, i32) else (n + 1) // 2
                piece = base[:, at[0]:at[0] + words]
                at[0] += words
                assert at[0] <= base.shape[1], at[0]
                return piece if dt == f32 else piece.bitcast(dt)[:, 0:n]
            return take

        take = carve(work)
        iota_k = take(128, bf16)
        iota_d = take(SD)
        lo2 = take(2 * NG, bf16).rearrange("p (g t) -> p g t", t=2)
        hi2 = take(2 * NG, bf16).rearrange("p (g t) -> p g t", t=2)
        ecode = take(SC * NS).rearrange("p (s c) -> p s c", c=SC)
        more = carve(rdeg)
        one_lo = [more(m * 128, bf16).rearrange("p (g k) -> p g k", g=m) for m in (8, 8, 10)]
        one_hi = [t(m * KW, bf16).rearrange("p (g k) -> p g k", g=m) for t, m in ((more, 8), (more, 8), (take, 10))]
        one_e_flat = take(SS * SC * SD)
        one_e = one_e_flat.rearrange("p (c s d) -> p s c d", s=SS, c=SC)
        xparts = take(NB * 2 * H, f16).rearrange("p (b f) -> p b f", b=NB)
        ering = take(SS * SC * H).rearrange("p (s c f) -> p s c f", s=SS, c=SC)
        gsum = more(STEP)
        estart_i = more(NS, i32)
        take = carve(work)
        parts = [take(NB * 2 * H, f16).rearrange("p (b f) -> p b f", b=NB) for _ in range(2)]
        H1 = take(NB * H).rearrange("p (b f) -> p b f", b=NB)
        agg = [take(TILE) for _ in range(2)]
        rz = take(4 * 2 * H).rearrange("p (b f) -> p b f", b=4)
        cand = take(4 * H).rearrange("p (b f) -> p b f", b=4)
        rest = take(4 * H).rearrange("p (b f) -> p b f", b=4)
        bst = take(6 * 4).rearrange("p (b s) -> p b s", b=4)
        rdiag = take(TILE).rearrange("p (b c) -> p b c", c=P)
        take = carve(big)
        dst_i = take(EC + 1, i32)
        src_i = take(EC, i32)
        dst_f, src_f = take(EC + 1), take(EC)
        q5, hi_f, tmp_f, key = take(EC), take(EC), take(EC), take(EC)
        last_start = take(6)
        thr = take(6)
        gbase = take(NG)
        sbase = take(NS)
        diag = take(128)
        cnt_row, row_f, ptr_f = take(6), take(6), take(6)
        row_i, ptr_i = take(6, i32), take(6, i32)
        found_i = take(6 * EC, i32).rearrange("p (j c) -> p j c", j=6)
        found_f = take(6 * EC).rearrange("p (j c) -> p j c", j=6)
        kwin = take(5 * WIN).rearrange("p (j c) -> p j c", j=5)
        ewin_i = take(SWIN, i32)
        ewin_f = take(SWIN)
        key_i, lo_i, hi_i = take(NG, i32), take(NG, i32), take(NG, i32)
        hi_c, ok_g = take(NG), take(NG)
        ok_e = take(SC * NS).rearrange("p (s c) -> p s c", c=SC)
        xsq = take(NB * H).rearrange("p (b f) -> p b f", b=NB)
        same, step1 = take(EC), take(EC)
        stats, bad, bad1 = take(5), take(5), take(1)
        w0_in = take(2 * H)
        wm_in = [take(3 * 2 * H).rearrange("p (c k) -> p c k", c=3) for _ in range(2)]
        wi_in = [take(3 * H) for _ in range(2)]
        wh_in = [take(3 * H) for _ in range(2)]
        bm_in = [take(1) for _ in range(2)]
        bi_in, bh_in = [take(3 * H) for _ in range(2)], [take(3 * H) for _ in range(2)]
        wmt = [take(4 * H) for _ in range(2)]
        bm3 = [take(3) for _ in range(2)]
        bias_f = [take(4 * H) for _ in range(2)]
        bpart = [take(4 * H, bf16) for _ in range(3)]
        bsel = take(4 * H)
        iota_n = take(N)
        one_n = take(N)
        sums = take(N)
        stage = take(2 * H)
        zero_st = take(2 * H)
        idx_now = take(1, i32)
        hneg = take(N)
        w_gen = [take(4 * H) for _ in range(2)]
        wg_l = [take(H + 1) for _ in range(2)]
        maskm1 = take(N)

        PS = ctx.enter_context(nc.psum_tensor("PS", [128, 8, 512], f32))

        def bank(b, cols=512, rows=128, n=1):
            return PS[0:rows, b, 0:cols] if n == 1 else PS[0:rows, b:b + n, 0:cols]

        one_eb = one_e_flat.bitcast(bf16).rearrange("p (c n t) -> p c n t", c=SC, t=2)
        W_LOADS = 16 * (2 + 2 * 6)
        key_dram = nc.dram_tensor("key_scratch", [E], f32).ap()
        h_dram = nc.dram_tensor("h_scratch", [N, H], f32).ap()
        out3 = out.rearrange("(b p) f -> p b f", p=P)
        h_dram3 = h_dram.rearrange("(b p) f -> p b f", p=P)

        dst_in, src_in, x_in, w_in = sem("dst_in"), sem("src_in"), sem("x_in"), sem("w_in")
        consts = sem("consts")
        first_diag, first_row = sem("first_diag"), sem("first_row")
        rows_ready, found = sem("rows_ready"), [sem("found_a"), sem("found_b")]
        key_ready, key_out = sem("key_ready"), sem("key_out")
        ptrs_ready, kwin_in, ewin_in = sem("ptrs_ready"), sem("kwin_in"), sem("ewin_in")
        ewin_ready, win_t, est_t = sem("ewin_ready"), sem("win_t"), sem("est_t")
        stats_ready, stats_sum, flag_ready = sem("stats_ready"), sem("stats_sum"), sem("flag_ready")
        wt_ready, wt_copied, wp_ready, w_done = sem("wt_ready"), sem("wt_copied"), sem("wp_ready"), sem("w_done")
        bias_ready, bias_c, bias_done = sem("bias_ready"), sem("bias_c"), sem("bias_done")
        lo_ready, lo2_done = sem("lo_ready"), sem("lo2_done")
        dve_c, act_c, pool_c = sem("dve_c"), sem("act_c"), sem("pool_c")
        one_ready = sem("one_ready")
        onee_ready = sem("onee_ready")
        unit_ready, unit_free = sem("unit_ready"), sem("unit_free")
        esum_ready, esum_free = sem("esum_ready"), sem("esum_free")
        e_in = [sem(f"e_in{i}") for i in range(SS)]
        e_used = sem("e_used")
        estart_ready = sem("estart_ready")
        parts_ready = sem("parts_ready")
        sweep_ready, agg_ready = sem("sweep_ready"), sem("agg_ready")
        gates_ready, gates_free = sem("gates_ready"), sem("gates_free")
        var_ready, std_ready = sem("var_ready"), sem("std_ready")
        rz_ready, cand_ready, tanh_ready = sem("rz_ready"), sem("cand_ready"), sem("tanh_ready")
        h_ready, rest_ready, rest_used = sem("h_ready"), sem("rest_ready"), sem("rest_used")
        ht_ready, he_ready = sem("ht_ready"), sem("he_ready")
        xhigh_ready, xrest_ready, x_whole = sem("xhigh_ready"), sem("xrest_ready"), sem("x_whole")
        rdiag_ready, gvar_ready, gstd_ready = sem("rdiag_ready"), sem("gvar_ready"), sem("gstd_ready")
        gsum_ready, gsum_copied, gcn_ready, gcn_used = sem("gsum_ready"), sem("gsum_copied"), sem("gcn_ready"), sem("gcn_used")
        gback_ready, gback_used = sem("gback_ready"), sem("gback_used")
        spread_ready, rdeg_ready, emean_ready = sem("spread_ready"), sem("rdeg_ready"), sem("emean_ready")
        idx_ok, estage_in = sem("idx_ok"), sem("estage_in")
        cand_used, w0t_ready = sem("cand_used"), sem("w0t_ready")
        y_ready, out_done = sem("y_ready"), sem("out_done")
        gen_c, stage_in, gone_ready, gused = sem("gen_c"), sem("stage_in"), sem("gone_ready"), sem("gused")
        pass_zeroed, pass_done, sums_ready = sem("pass_zeroed"), sem("pass_done"), sem("sums_ready")
        gz_ready, hstore, idx_set, neg_ready = sem("gz_ready"), sem("hstore"), sem("idx_set"), sem("neg_ready")

        block = ctx.enter_context(nc.Block())

        @block.sync
        def _(sp):
            sp.dma_start(dst_i[0:P, 0:EC], dst.rearrange("(p c) -> p c", c=EC)).then_inc(dst_in, 16)
            sp.wait_ge(consts, 1)
            sp.dma_start(dst_i[0:P - 1, EC:EC + 1], dst[EC:E].rearrange("(p c) -> p c", c=EC)[:, 0:1],
                         allow_slow_non_contiguous=True).then_inc(dst_in, 16)
            sp.dma_start(src_i[0:P, :], src.rearrange("(p c) -> p c", c=EC)).then_inc(src_in, 16)
            sp.dma_start(X0[0:P, :, :], x.rearrange("(b p) f -> p b f", p=P)).then_inc(x_in, 16)
            sp.wait_ge(key_ready, 1)
            sp.dma_start(key_dram.rearrange("(p c) -> p c", c=EC), key[0:P, :]).then_inc(key_out, 16)

            def load_windows(it, slots, wait):
                for k in range(0, slots, 4):
                    here = range(k, min(k + 4, slots))
                    _, starts = nc.values_load_multi_w_load_instructions(
                        estart_i[0:1, bass.ds(it * SS + k, len(here))], engines=[mybir.EngineType.SP],
                        min_val=0, max_val=E - SWIN)
                    for s, at in zip(here, starts):
                        if wait:
                            sp.wait_ge(e_used, it * SS + (s + 1 - SS))
                        sp.dma_start(ering[:, s, :, :],
                                     e[bass.ds(at, SWIN), :].rearrange("(p c) f -> p c f", c=SC)
                                     ).then_inc(e_in[s], 16)

            def usual():
                sp.wait_ge(estart_ready, 1)
                load_windows(0, SS, False)
                with sp.Fori(1, ITS) as it:
                    load_windows(it, SS, True)
                load_windows(ITS, LS, True)

            def general():
                sp.wait_ge(gz_ready, 2)
                e3 = e.rearrange("(p c) f -> p c f", c=EC)
                with sp.Fori(0, EC) as c:
                    sp.wait_ge(gused, c + (EC + 1))
                    sp.dma_start(stage[0:P, H:2 * H], e3[:, bass.ds(c, 1), :].rearrange("p c f -> p (c f)")
                                 ).then_inc(estage_in, 16)
                for r, hbuf in ((1, X0), (2, H1)):
                    sp.wait_ge(h_ready, NT * r)
                    sp.dma_start(h_dram3, hbuf[0:P, :, :]).then_inc(hstore, 16)
                    sp.wait_ge(hstore, 16 * r)

            sp.wait_ge(flag_ready, 1)
            bad_inputs = sp.value_load(flag[0:1, 0:1], min_val=0, max_val=5)
            with sp.If(bad_inputs == 0):
                usual()
            with sp.Else():
                general()
            sp.wait_ge(y_ready, 1)
            sp.dma_start(out3, H1[0:P, :, :]).then_inc(out_done, 16)
            sp.wait_ge(out_done, 16)

        @block.gpsimd
        def _(pool):
            pool.memset(dst_i[:, EC:EC + 1], N).then_inc(consts, 1)
            pool.memset(ones[:, :], 1.0).then_inc(consts, 1)
            pool.memset(onesb[:, :], 1.0).then_inc(consts, 1)
            pool.memset(ident[:, :], 0.0).then_inc(pool_c, 1)
            pool.wait_ge(pool_c, 1)
            pool.affine_select(out=ident[:, :], in_=ident[:, :], compare_op=ALU.not_equal, fill=1.0, base=0,
                               pattern=[[-1, 128]], channel_multiplier=1).then_inc(consts, 1)
            pool.iota(thr[:, 0:5], pattern=[[GD * P, 5]], base=0, channel_multiplier=GD,
                      allow_small_or_imprecise_dtypes=True).then_inc(consts, 1)
            pool.iota(thr[:, 5:6], pattern=[[0, 1]], base=0, channel_multiplier=SD,
                      allow_small_or_imprecise_dtypes=True).then_inc(consts, 1)
            pool.memset(last_start[:, 0:5], float(E - WIN)).then_inc(consts, 1)
            pool.memset(last_start[:, 5:6], float(E - SWIN)).then_inc(consts, 1)
            pool.memset(stats, 0.0).then_inc(consts, 1)
            pool.memset(loscale[0:H, :], 1.0).then_inc(consts, 1)
            pool.wait_ge(consts, 10)
            pool.memset(loscale[H:128, :], 1.0 / LO).then_inc(consts, 1)
            for r in range(2):
                pool.memset(w_he[r][H:128, 3 * H:4 * H], 0.0).then_inc(consts, 1)
            pool.wait_ge(consts, 13)
            pool.memset(eps_col[:, :], EPS).then_inc(consts, 1)
            pool.iota(iota_k, pattern=[[1, 128]], base=0, channel_multiplier=0,
                      allow_small_or_imprecise_dtypes=True).then_inc(consts, 1)
            pool.iota(iota_d, pattern=[[1, SD]], base=0, channel_multiplier=0,
                      allow_small_or_imprecise_dtypes=True).then_inc(consts, 1)
            for two in one_lo:
                pool.memset(two[:, :, KW:128], 0.0).then_inc(consts, 1)
            for j, total in enumerate((E, E, N, E - N, N * H)):
                pool.memset(bad[0:1, j:j + 1], float(total)).then_inc(consts, 1)
            pool.wait_ge(rows_ready, 1)
            dst_rows = dst.rearrange("(r c) -> r c", c=EC)
            for j in range(6):
                pool.indirect_dma_start(out=found_i[0:P, j, :], out_offset=None, in_=dst_rows,
                                        in_offset=bass.IndirectOffsetOnAxis(ap=row_i[0:P, j:j + 1], axis=0)
                                        ).then_inc(found[j // 3], 16)
            pool.wait_ge(key_out, 16)
            key_rows = key_dram.rearrange("(n o) -> n o", o=1)
            for j in range(5):
                if j % 3 == 0:
                    pool.wait_ge(ptrs_ready, j // 3 + 1)
                pool.indirect_dma_start(out=kwin[0:P, j, :], out_offset=None, in_=key_rows,
                                        in_offset=bass.IndirectOffsetOnAxis(ap=ptr_i[0:P, j:j + 1], axis=0)
                                        ).then_inc(kwin_in, 16)
            pool.indirect_dma_start(out=ewin_i[0:P, :], out_offset=None, in_=dst.rearrange("(n o) -> n o", o=1),
                                    in_offset=bass.IndirectOffsetOnAxis(ap=ptr_i[0:P, 5:6], axis=0)
                                    ).then_inc(ewin_in, 16)
            pool.iota(gbase, pattern=[[P, NG]], base=0, channel_multiplier=0,
                      allow_small_or_imprecise_dtypes=True).then_inc(consts, 1)
            pool.iota(sbase, pattern=[[SD, NS]], base=0, channel_multiplier=0,
                      allow_small_or_imprecise_dtypes=True).then_inc(consts, 1)
            bc = Chain(pool, bias_c)
            for r in range(2):
                pool.wait_ge(bias_ready, r + 1)
                bf = bias_f[r][0:3, :]
                for k in range(3):
                    bc.done(pool.tensor_copy(bpart[k][0:3, :], bf))
                    if k < 2:
                        bc.done(nc.gpsimd.tensor_tensor(bf, bf, bpart[k][0:3, :], ALU.subtract))
                for k in range(3):
                    to = bf if k else bsel[0:3, :]
                    bc.done(nc.gpsimd.tensor_tensor(to, bpart[k][0:3, :], ident[0:3, k:k + 1].to_broadcast([3, 4 * H]), ALU.mult))
                    if k:
                        bc.done(nc.gpsimd.tensor_tensor(bsel[0:3, :], bsel[0:3, :], bf, ALU.add))
                pool.tensor_copy(bias3[r][0:3, :], bsel[0:3, :]).then_inc(bias_done, 1)
                pool.wait_ge(bias_done, r + 1)

            def general():
                pool.iota(iota_n, pattern=[[1, N]], base=0, channel_multiplier=0,
                          allow_small_or_imprecise_dtypes=True).then_inc(gz_ready, 1)
                pool.memset(zero_st, 0.0).then_inc(pass_zeroed, 1)
                pool.memset(stage, 1.0).then_inc(pass_zeroed, 1)
                pool.wait_ge(gused, EC + 1)
                pool.memset(stage[:, 0:H], 0.0).then_inc(gz_ready, 1)
                pool.wait_ge(gused, 2 * EC + 1)
                pool.memset(stage[:, H:2 * H], 0.0).then_inc(gz_ready, 1)
                for r in range(3):
                    if r:
                        pool.wait_ge(hstore, 16 * r)
                    table = x if r == 0 else h_dram
                    with pool.Fori(0, EC) as c:
                        pool.wait_ge(gused, c + ((2 + r) * EC + 1))
                        pool.tensor_copy(idx_now[0:P, :], src_i[0:P, bass.ds(c, 1)]).then_inc(idx_set, 1)
                        pool.wait_ge(idx_set, c + (r * EC + 1))
                        pool.sem_inc(idx_ok, 1)
                        pool.indirect_dma_start(out=stage[0:P, 0:H], out_offset=None, in_=table,
                                                in_offset=bass.IndirectOffsetOnAxis(ap=idx_now[0:P, 0:1], axis=0)
                                                ).then_inc(stage_in, 16)

            pool.wait_ge(flag_ready, 1)
            bad_inputs = pool.value_load(flag[0:1, 0:1], min_val=0, max_val=5)
            with pool.If(bad_inputs == 0):
                pool.tensor_copy(xparts[0:P, :, 0:H], X0[0:P, :, :]).then_inc(xhigh_ready, 1)
                pool.wait_ge(xhigh_ready, 1)
                nc.gpsimd.tensor_tensor(X0[0:P, :, :], X0[0:P, :, :], xparts[0:P, :, 0:H], ALU.subtract
                                        ).then_inc(xrest_ready, 1)
                pool.wait_ge(parts_ready, 1)
                nc.gpsimd.tensor_tensor(X0[0:P, :, :], X0[0:P, :, :], xparts[0:P, :, 0:H], ALU.add
                                        ).then_inc(x_whole, 1)
                for t in range(NT):
                    cols = slice(TILE * t, TILE * t + len(blocks_of(t)) * P)
                    pool.wait_ge(rdeg_ready, t + 1)
                    nc.gpsimd.tensor_tensor(HE[H:128, cols], HE[H:128, cols], rdeg[H:128, cols], ALU.mult
                                            ).then_inc(emean_ready, 1)
            with pool.Else():
                general()

        @block.vector
        def _(dve):
            ch = Chain(dve, dve_c)
            v = nc.vector
            MAGIC = 12582912.0

            dve.wait_ge(dst_in, 32)
            ch.done(v.tensor_copy(dst_f[0:P, :], dst_i[0:P, :]))
            dve.wait_ge(consts, 24)
            v.tensor_scalar(diag[0:P, 0:P], ident[0:P, 0:P], dst_f[0:P, 0:1], None, ALU.mult).then_inc(first_diag, 1)
            ch.done(v.tensor_scalar(q5[0:P, :], dst_f[0:P, 0:EC], 0.2, -0.4, ALU.mult, ALU.add))
            ch.done(v.tensor_scalar(q5[0:P, :], q5[0:P, :], MAGIC, -MAGIC, ALU.add, ALU.add))
            dve.wait_ge(first_row, 1)
            for j in range(6):
                ch.add(v.tensor_scalar(found_f[0:P, j, 0:P], bank(0, P, P), thr[0:P, j:j + 1], None, ALU.is_lt,
                                       ALU.add, accum_out=cnt_row[0:P, j:j + 1]))
            ch.wait()
            ch.done(v.tensor_scalar(row_f[0:P, :], cnt_row[0:P, :], -1.0, 0.0, ALU.add, ALU.max))
            v.tensor_copy(row_i[0:P, :], row_f[0:P, :]).then_inc(rows_ready, 1)
            dve.wait_ge(src_in, 16)
            ch.done(v.tensor_copy(src_f[0:P, :], src_i[0:P, :]))
            ch.done(v.tensor_scalar(hi_f[0:P, :], src_f[0:P, :], 1.0 / P, -(P - 1) / 2.0 / P, ALU.mult, ALU.add))
            ch.done(v.tensor_scalar(hi_f[0:P, :], hi_f[0:P, :], MAGIC, -MAGIC, ALU.add, ALU.add))
            ch.done(v.scalar_tensor_tensor(src_f[0:P, :], hi_f[0:P, :], -float(P), src_f[0:P, :], ALU.mult, ALU.add))
            ch.done(v.scalar_tensor_tensor(tmp_f[0:P, :], hi_f[0:P, :], float(GD), dst_f[0:P, 0:EC], ALU.mult, ALU.add))
            ch.done(v.scalar_tensor_tensor(tmp_f[0:P, :], q5[0:P, :], float(NB * GD - GD), tmp_f[0:P, :], ALU.mult, ALU.add))
            v.scalar_tensor_tensor(key[0:P, :], tmp_f[0:P, :], 128.0, src_f[0:P, :], ALU.mult, ALU.add).then_inc(key_ready, 1)
            for k in range(2):
                dve.wait_ge(found[k], 3 * 16)
                cols = slice(3 * k, 3 * k + 3)
                for j in range(3 * k, 3 * k + 3):
                    ch.add(v.tensor_scalar(found_f[0:P, j, :], found_i[0:P, j, :], thr[0:P, j:j + 1], None, ALU.is_lt,
                                           ALU.add, accum_out=cnt_row[0:P, j:j + 1]))
                ch.wait()
                ch.done(v.scalar_tensor_tensor(ptr_f[0:P, cols], row_f[0:P, cols], float(EC), cnt_row[0:P, cols],
                                               ALU.mult, ALU.add))
                ch.done(v.tensor_tensor(ptr_f[0:P, cols], ptr_f[0:P, cols], last_start[0:P, cols], ALU.min))
                v.tensor_copy(ptr_i[0:P, cols], ptr_f[0:P, cols]).then_inc(ptrs_ready, 1)

            ch.done(v.tensor_tensor(same[0:P, :], dst_f[0:P, 1:EC + 1], dst_f[0:P, 0:EC], ALU.subtract))
            ch.done(v.tensor_scalar(step1[0:P, :], same[0:P, :], 1.0, None, ALU.is_equal, ALU.add,
                                    accum_out=stats[0:P, 2:3]))
            ch.done(v.tensor_scalar(step1[0:P, :], same[0:P, :], 0.0, None, ALU.is_equal, ALU.add,
                                    accum_out=stats[0:P, 3:4]))
            dve.wait_ge(x_in, 16)
            ch.done(v.tensor_tensor(xsq[0:P, :, :], X0[0:P, :, :], X0[0:P, :, :], ALU.mult))
            ch.done(v.tensor_scalar(xsq[0:P, :, :], xsq[0:P, :, :], XMAX2, None, ALU.is_le, ALU.add,
                                    accum_out=stats[0:P, 4:5]))
            dve.wait_ge(est_t, 1)
            v.tensor_copy(estart_i[0:1, :], bank(3, NS, 1)).then_inc(estart_ready, 1)
            dve.wait_ge(ewin_in, 16)
            v.tensor_copy(ewin_f[0:P, :], ewin_i[0:P, :]).then_inc(ewin_ready, 1)

            dve.wait_ge(win_t, 1)
            ch.done(v.tensor_copy(key_i[:, 0:500], bank(0, 500)))
            ch.done(v.tensor_copy(key_i[:, 500:NG], bank(1, NG - 500)))
            dve.wait_ge(consts, 26)
            ch.done(v.tensor_scalar(lo_i, key_i, 127, None, ALU.bitwise_and))
            ch.done(v.tensor_scalar(hi_i, key_i, 7, None, ALU.logical_shift_right))
            dve.sem_inc(lo_ready, 1)
            ch.done(v.tensor_tensor(hi_c, hi_i, gbase, ALU.subtract))
            v.tensor_copy(hi2, hi_c.unsqueeze(2).to_broadcast([128, NG, 2]))
            ch.done(v.tensor_scalar(ok_g, hi_c, 0.0, None, ALU.is_ge))
            ch.done(v.scalar_tensor_tensor(hi_c, hi_c, float(NB * GD), ok_g, ALU.is_lt, ALU.mult,
                                           accum_out=stats[:, 0:1]))
            dve.wait_ge(win_t, 2)
            ch.done(v.tensor_tensor(ecode, bank(2, SC * NS).rearrange("p (c s) -> p s c", c=SC),
                                    sbase.unsqueeze(2).to_broadcast([128, NS, SC]), ALU.subtract))
            ch.done(v.tensor_scalar(ok_e, ecode, 0.0, None, ALU.is_ge))
            ch.done(v.scalar_tensor_tensor(ok_e, ecode, float(SD), ok_e, ALU.is_lt, ALU.mult,
                                           accum_out=stats[:, 1:2]))
            dve.sem_inc(stats_ready, 1)
            dve.wait_ge(lo2_done, 1)
            dve.wait_ge(stats_sum, 1)
            ch.done(v.tensor_tensor(bad[0:1, :], bank(3, 5, 1), bad[0:1, :], ALU.not_equal))
            ch.done(v.tensor_reduce(bad1[0:1, :], bad[0:1, :], mybir.AxisListType.X, ALU.add))
            v.tensor_copy(flag[0:1, :], bad1[0:1, :]).then_inc(flag_ready, 1)

            def one_hots(it, i, ng):
                first, size = BATCHES[i]
                m = min(size, ng - first)
                if m <= 0:
                    return
                dve.wait_ge(unit_ready, it * SU + (UCREDIT + (2 * (i - 2) if i > 2 else (-5, -3, 0)[i])))
                for two, codes in ((one_lo[i % 3], lo2), (one_hi[i % 3], hi2)):
                    v.tensor_tensor(
                        two[:, 0:m, 0:KW].rearrange("p g (k t) -> p g k t", t=2),
                        codes[:, bass.ds(it * SG + first, m), :].unsqueeze(2).to_broadcast([128, m, KW // 2, 2]),
                        iota_k[:, 0:KW].rearrange("p (k t) -> p k t", t=2).unsqueeze(1).to_broadcast([128, m, KW // 2, 2]),
                        ALU.is_equal).then_inc(one_ready, 1)

            def one_es(it, ns):
                dve.wait_ge(esum_ready, it + 1)
                for k in range(0, ns, 5):
                    v.tensor_tensor(one_e[:, k:k + 5, :, :],
                                    ecode[:, bass.ds(it * SS + k, 5), :].unsqueeze(3).to_broadcast([128, 5, SC, SD]),
                                    iota_d.unsqueeze(1).unsqueeze(1).to_broadcast([128, 5, SC, SD]),
                                    ALU.is_equal).then_inc(onee_ready, 1)

            def build_step(it, ng, ns):
                for i in range(6):
                    one_hots(it, i, ng)
                    if i == 1:
                        one_es(it, ns)

            def spread(t):
                blks = blocks_of(t)
                if t:
                    dve.wait_ge(spread_ready, t)
                v.tensor_tensor(rdiag[0:P, 0:len(blks), :], ident[0:P, 0:P].unsqueeze(1).to_broadcast([P, len(blks), P]),
                                rnode[0:P, blks[0]:blks[-1] + 1].unsqueeze(2).to_broadcast([P, len(blks), P]),
                                ALU.mult).then_inc(rdiag_ready, 1)

            def mean(S, t, gen):
                if S < NT and not gen:
                    dve.wait_ge(rdeg_ready, t + 1)
                w = len(blocks_of(t)) * P
                if S >= 2:
                    dve.wait_ge(gates_ready, S - 1)
                if gen:
                    from_ = sums[:, TILE * t:TILE * t + w]
                else:
                    dve.wait_ge(sweep_ready, S + 1)
                    from_ = bank(S % 2, w)
                v.tensor_tensor(agg[S % 2][:, 0:w], from_, rdeg[:, TILE * t:TILE * t + w], ALU.mult
                                ).then_inc(agg_ready, 1)

            def moments(y, t):
                for i, b in enumerate(blocks_of(t)):
                    ch.add(v.bn_stats(bst[0:P, i, :], y[0:P, b, :]))
                ch.wait()
                for i, b in enumerate(blocks_of(t)):
                    ch.add(v.bn_aggr(mv[0:P, b, :], bst[0:P, i, :]))
                ch.wait()

            def normalize(y, blks):
                for b in blks:
                    ch.add(v.tensor_scalar(y[0:P, b, :], y[0:P, b, :], mv[0:P, b, 0:1], rstd[0:P, b:b + 1],
                                           ALU.subtract, ALU.mult))
                ch.wait()

            def hand_over(k, h, t, gen):
                T = NT * k + t
                blks = blocks_of(t)
                sl = slice(blks[0], blks[-1] + 1)
                if gen:
                    dve.sem_inc(h_ready, 1)
                    return
                p = parts[k]
                v.tensor_copy(p[0:P, sl, 0:H], h[0:P, sl, :]).then_inc(h_ready, 1)
                dve.wait_ge(h_ready, T + 1)
                if T >= 1:
                    dve.wait_ge(rest_used, T)
                v.tensor_tensor(rest[0:P, 0:len(blks), :], h[0:P, sl, :], p[0:P, sl, 0:H], ALU.subtract
                                ).then_inc(rest_ready, 1)

            def x_plus_gcn(t):
                blks = blocks_of(t)
                n, sl = len(blks), slice(blks[0], blks[-1] + 1)
                dve.wait_ge(gback_ready, t + 1)
                ch.done(v.tensor_tensor(cand[0:P, 0:n, :], bank(2 + t % 2, n * H, P).rearrange("p (b f) -> p b f", f=H),
                                        rnode[0:P, sl].unsqueeze(2).to_broadcast([P, n, H]), ALU.mult))
                dve.sem_inc(gback_used, 1)
                ch.done(v.tensor_tensor(X0[0:P, sl, :], X0[0:P, sl, :], cand[0:P, 0:n, :], ALU.add))
                moments(X0, t)
                v.tensor_copy(rstd[0:P, sl], mv[0:P, sl, 1]).then_inc(gvar_ready, 1)

            def gcn(t):
                blks = blocks_of(t)
                n, sl = len(blks), slice(blks[0], blks[-1] + 1)
                dve.wait_ge(gates_ready, t + 1)
                v.tensor_tensor(X0[0:P, sl, :], X0[0:P, sl, :],
                                bank(2 + 2 * (t % 2), n * H, P).rearrange("p (b f) -> p b f", f=H), ALU.add
                                ).then_inc(gates_free, 1)
                dve.wait_ge(gates_free, t + 1)
                moments(X0, t)
                v.tensor_copy(rstd[0:P, sl], mv[0:P, sl, 1]).then_inc(var_ready, 1)
                dve.wait_ge(std_ready, t + 1)
                ch.done(v.reciprocal(rstd[0:P, sl], rstd[0:P, sl]))
                normalize(X0, blks)
                hand_over(0, X0, t, True)

            def gru(r, t, gen):
                S, G, blks = NT * (r + gen) + t, NT * r + t, blocks_of(t)
                n, sl = len(blks), slice(blks[0], blks[-1] + 1)
                old = X0 if r == 0 else H1
                gates = bank(2 + 2 * (S % 2), 512, P, 2).rearrange("p a (b f) -> p (a b) f", b=2)
                dve.wait_ge(rz_ready, G + 1)
                ch.done(v.tensor_tensor(cand[0:P, 0:n, :], rz[0:P, 0:n, 0:H], gates[:, 0:n, 3 * H:4 * H], ALU.mult))
                v.tensor_tensor(cand[0:P, 0:n, :], cand[0:P, 0:n, :], gates[:, 0:n, 2 * H:3 * H], ALU.add
                                ).then_inc(gates_free, 1)
                dve.wait_ge(tanh_ready, G + 1)
                ch.done(v.tensor_tensor(H1[0:P, sl, :], old[0:P, sl, :], cand[0:P, 0:n, :], ALU.subtract))
                ch.done(v.tensor_tensor(H1[0:P, sl, :], H1[0:P, sl, :], rz[0:P, 0:n, H:2 * H], ALU.mult))
                v.tensor_tensor(H1[0:P, sl, :], H1[0:P, sl, :], cand[0:P, 0:n, :], ALU.add).then_inc(cand_used, 1)
                dve.wait_ge(cand_used, G + 1)
                if r == 0:
                    hand_over(1, H1, t, gen)
                else:
                    ch.done(v.tensor_tensor(H1[0:P, sl, :], H1[0:P, sl, :], X0[0:P, sl, :], ALU.add))
                    moments(H1, t)

            def rounds(gen):
                if gen:
                    for t in range(NT):
                        mean(t, t, gen)
                        gcn(t)
                for r in range(2):
                    if gen:
                        neg_h(r)
                        general_pass(3 + r)
                    for t in range(NT):
                        mean(NT * (r + gen) + t, t, gen)
                        if r == 0 and t + 1 < NT and not gen:
                            spread(t + 1)
                        gru(r, t, gen)
                v.tensor_copy(rstd[0:P, :], mv[0:P, :, 1]).then_inc(var_ready, 1)
                dve.wait_ge(std_ready, NT + 1 if gen else 1)
                ch.done(v.reciprocal(rstd[0:P, :], rstd[0:P, :]))
                normalize(H1, range(NB))
                dve.sem_inc(y_ready, 1)

            def usual():
                with dve.Fori(0, ITS) as it:
                    build_step(it, SG, SS)
                build_step(ITS, LG, LS)
                dve.wait_ge(gcn_used, ITS)
                ch.done(v.reciprocal(rnode[0:P, 0:NB - 1], rnode[0:P, 0:NB - 1]))
                dve.wait_ge(unit_ready, UCREDIT + SU * ITS + LU)
                dve.wait_ge(esum_ready, ITS + 2)
                dve.wait_ge(x_whole, 1)
                x_plus_gcn(0)
                for t in range(NT):
                    if t + 2 == NT:
                        dve.wait_ge(gcn_used, ITS + 1)
                        ch.done(v.reciprocal(rnode[0:P, NB - 1:NB], rnode[0:P, NB - 1:NB]))
                    if t + 1 < NT:
                        x_plus_gcn(t + 1)
                    sl = slice(blocks_of(t)[0], blocks_of(t)[-1] + 1)
                    dve.wait_ge(gstd_ready, t + 1)
                    ch.done(v.reciprocal(rstd[0:P, sl], rstd[0:P, sl]))
                    normalize(X0, blocks_of(t))
                    hand_over(0, X0, t, False)
                    if t == 4:
                        spread(0)
                rounds(False)

            def general_pass(q):
                with dve.Fori(0, EC) as c:
                    dve.wait_ge(gused, c + (q * EC + 1))
                    v.tensor_scalar(one_n[0:P, :], iota_n[0:P, :], dst_f[0:P, bass.ds(c, 1)], None, ALU.is_equal
                                    ).then_inc(gone_ready, 1)
                dve.wait_ge(pass_done, q + 1)
                for t in range(NT):
                    w = len(blocks_of(t)) * P
                    ch.add(v.tensor_copy(sums[:, TILE * t:TILE * t + w], bank(t, w)))
                ch.wait()
                dve.sem_inc(sums_ready, 1)

            def neg_h(r):
                dve.wait_ge(he_ready, NT * (r + 1))
                ch.done(v.tensor_tensor(hneg[0:H, :], maskm1[0:H, :], HE[0:H, :], ALU.mult))
                v.tensor_copy(hneg[H:H + 1, :], maskm1[H:H + 1, :]).then_inc(neg_ready, 1)

            def general():
                dve.wait_ge(gz_ready, 1)
                for r in range(2):
                    ch.done(v.tensor_copy(wg_l[r][:, 0:H], wmt[r][:, 0:H]))
                    v.tensor_copy(wg_l[r][:, H:H + 1], bm_in[r]).then_inc(gen_c, 1)
                for r in range(2):
                    dve.wait_ge(gen_c, 3 + r)
                    ch.done(v.tensor_copy(w_gen[r][0:H + 1, 0:3 * H], bank(r, 3 * H, H + 1)))
                    v.memset(w_gen[r][0:H + 1, 3 * H:4 * H], 0.0).then_inc(neg_ready, 1)
                general_pass(0)
                ch.done(v.tensor_scalar(maskm1, sums, 1.0, -1.0, ALU.min, ALU.add))
                ch.done(v.tensor_scalar(sums, sums, 1.0, None, ALU.max))
                ch.done(v.reciprocal(rdeg[:, :], sums))
                general_pass(1)
                ch.done(v.tensor_tensor(HE[H:128, :], sums[H:128, :], rdeg[H:128, :], ALU.mult))
                general_pass(2)
                rounds(True)

            dve.wait_ge(flag_ready, 1)
            bad_inputs = dve.value_load(flag[0:1, 0:1], min_val=0, max_val=5)
            base = ch.n
            with dve.If(bad_inputs == 0):
                usual()
            ch.n = base
            with dve.Else():
                general()

        @block.scalar
        def _(act):
            a = nc.scalar
            for half in range(2):
                act.dma_start(w0_in[0:H, half * H:(half + 1) * H], w0).then_inc(w_in, 16)
            for r in range(2):
                act.dma_start(wm_in[r][0:H, :, :], w_msg[r].rearrange("(c p) k -> p c k", p=H)).then_inc(w_in, 16)
                act.dma_start(wi_in[r], w_ih[r]).then_inc(w_in, 16)
                act.dma_start(wh_in[r][0:H, :], w_hh[r]).then_inc(w_in, 16)
                act.dma_start(bm_in[r], b_msg[r].rearrange("(k o) -> k o", o=1)).then_inc(w_in, 16)
                act.dma_start(bi_in[r][0:1, :], b_ih[r:r + 1, :]).then_inc(w_in, 16)
                act.dma_start(bh_in[r][0:1, :], b_hh[r:r + 1, :]).then_inc(w_in, 16)
            act.wait_ge(w_in, W_LOADS)
            for r in range(2):
                act.activation(bm3[r], bm_in[r].to_broadcast([128, 3]), ACT.Copy).then_inc(act_c, 1)
                act.wait_ge(wt_ready, r + 1)
                act.activation(wmt[r], bank(6 + r, 4 * H), ACT.Copy).then_inc(wt_copied, 1)
            for r in range(2):
                act.wait_ge(wp_ready, r + 1)
                act.activation(bias_f[r][0:3, :], bank(5, 4 * H, 3), ACT.Copy).then_inc(bias_ready, 1)
                act.activation(w_he[r][:, 0:3 * H], bank(4, 3 * H), ACT.Copy)
                act.activation(w_he[r][0:H, 3 * H:4 * H], wh_in[r][0:H, 2 * H:3 * H], ACT.Copy)
                act.activation(w_ag[r][:, :], bank(7, 3 * H), ACT.Copy, scale=loscale[:, 0:1]).then_inc(w_done, 1)
            act.wait_ge(w0t_ready, 1)
            act.activation(w0t[:, :], bank(6, H), ACT.Copy, scale=loscale[:, 0:1]).then_inc(w_done, 1)
            act.wait_ge(lo_ready, 1)
            act.activation(lo2, lo_i.unsqueeze(2).to_broadcast([128, NG, 2]), ACT.Copy).then_inc(lo2_done, 1)

            def unit(it, u, n):
                act.wait_ge(unit_ready, it * SU + (u + 1 + UCREDIT))
                act.activation(
                    A3[:, :, bass.ds(it * STEP + 20 * u, n * GD)].rearrange("p s (g d) -> p s g d", g=n),
                    bank(UBANK[u % 5], n * P).rearrange("p (g s d) -> p s g d", g=n, d=GD), ACT.Copy
                ).then_inc(unit_free, 1)

            def edge_sums(it, ns):
                act.wait_ge(esum_ready, it + 2)
                act.activation(HE[H:128, bass.ds(it * STEP, ns * SD)], PS[H:128, 5, 0:ns * SD], ACT.Copy
                               ).then_inc(esum_free, 1)

            def gcn_sums(i, nb):
                act.wait_ge(gsum_ready, i + 1)
                act.activation(gsum[:, 0:nb * P], bank(7, nb * P), ACT.Copy).then_inc(gsum_copied, 1)

            def gcn_out(i, nb):
                act.wait_ge(gcn_ready, i + 1)
                act.activation(HE[0:H, bass.ds(i * STEP, nb * P)], bank(4, nb * P, H), ACT.Copy)
                act.activation(rnode[0:P, bass.ds(i * 2, nb)], bank(4)[0:P, STEP:STEP + nb], ACT.Copy).then_inc(gcn_used, 1)

            def build_step(it, units, ng, ns, prev):
                for u in range(units):
                    if u == 4 and prev:
                        gcn_sums(it - 1, 2)
                    if u == 7 and prev:
                        gcn_out(it - 1, 2)
                    unit(it, u, min(4, ng - 4 * u))
                if units == 7:
                    gcn_out(it - 1, 2)
                edge_sums(it, ns)

            def hand_over(k, t, gen):
                T, blks = NT * k + t, blocks_of(t)
                n, w, sl = len(blks), len(blks) * P, slice(blks[0], blks[-1] + 1)
                if not gen:
                    act.wait_ge(rest_ready, T + 1)
                    a.activation(parts[k][0:P, sl, H:2 * H], rest[0:P, 0:n, :], ACT.Copy,
                                 scale=LO).then_inc(rest_used, 1)
                act.wait_ge(ht_ready, T + 1)
                a.activation(HE[0:H, TILE * t:TILE * t + w], bank(6, w, H), ACT.Copy).then_inc(he_ready, 1)

            def rounds(gen):
                def spread(t):
                    w = len(blocks_of(t)) * P
                    act.wait_ge(spread_ready, t + 1)
                    a.activation(rdeg[:, TILE * t:TILE * t + w], bank(7, w), ACT.Copy).then_inc(rdeg_ready, 1)

                def std(t, var, done):
                    sl = slice(blocks_of(t)[0], blocks_of(t)[-1] + 1)
                    act.wait_ge(var, t + 1)
                    a.activation(rstd[0:P, sl], rstd[0:P, sl], ACT.Sqrt, bias=eps_col[0:P, 0:1]).then_inc(done, 1)

                if not gen:
                    std(0, gvar_ready, gstd_ready)
                for t in range(NT):
                    if gen:
                        std(t, var_ready, std_ready)
                    elif t + 1 < NT:
                        std(t + 1, gvar_ready, gstd_ready)
                    hand_over(0, t, gen)
                    if t == 4 and not gen:
                        spread(0)
                for r in range(2):
                    for t in range(NT):
                        S, G, n = NT * (r + gen) + t, NT * r + t, len(blocks_of(t))
                        gates = bank(2 + 2 * (S % 2), 512, P, 2).rearrange("p a (b f) -> p (a b) f", b=2)
                        if r == 0 and t + 1 < NT and not gen:
                            spread(t + 1)
                        act.wait_ge(gates_ready, S + 1)
                        if G > 0:
                            act.wait_ge(cand_used, G)
                        a.activation(rz[0:P, 0:n, :], gates[:, 0:n, 0:2 * H], ACT.Sigmoid).then_inc(rz_ready, 1)
                        act.wait_ge(gates_free, S + 1)
                        a.activation(cand[0:P, 0:n, :], cand[0:P, 0:n, :], ACT.Tanh).then_inc(tanh_ready, 1)
                        if r == 0:
                            hand_over(1, t, gen)
                act.wait_ge(var_ready, NT + 1 if gen else 1)
                a.activation(rstd[0:P, :], rstd[0:P, :], ACT.Sqrt, bias=eps_col[0:P, 0:1]).then_inc(std_ready, 1)

            def usual():
                act.sem_inc(unit_free, 5)
                act.sem_inc(esum_free, 1)
                build_step(0, SU, SG, SS, False)
                act.wait_ge(xrest_ready, 1)
                act.activation(xparts[0:P, :, H:2 * H], X0[0:P, :, :], ACT.Copy, scale=LO).then_inc(parts_ready, 1)
                with act.Fori(1, ITS) as it:
                    build_step(it, SU, SG, SS, True)
                build_step(ITS, LU, LG, LS, True)
                gcn_sums(ITS, 1)
                gcn_out(ITS, 1)
                rounds(False)

            act.wait_ge(flag_ready, 1)
            bad_inputs = act.value_load(flag[0:1, 0:1], min_val=0, max_val=5)
            with act.If(bad_inputs == 0):
                usual()
            with act.Else():
                rounds(True)

        @block.tensor
        def _(pe):
            mm = nc.tensor.matmul

            pe.wait_ge(first_diag, 1)
            mm(bank(0, P, P), ones[0:P, 0:P], diag[0:P, 0:P], start=True, stop=True).then_inc(first_row, 1)
            pe.wait_ge(w_in, W_LOADS)
            for r in range(2):
                for k, c in enumerate((0, 2, 1, 1)):
                    ins = nc.tensor.transpose(bank(6 + r, 4 * H)[:, k * H:(k + 1) * H], wm_in[r][0:H, c, :],
                                              ident[0:H, 0:H])
                ins.then_inc(wt_ready, 1)
            pe.wait_ge(wt_copied, 2)
            nc.tensor.transpose(bank(6, H), w0_in[0:H, :], ident[0:H, 0:H]).then_inc(w0t_ready, 1)
            for r in range(2):
                if r:
                    pe.wait_ge(w_done, 1)
                rz_cols, n_cols = slice(0, 2 * H), slice(2 * H, 3 * H)
                mm(bank(4)[:, rz_cols], wmt[r][:, 0:2 * H], wi_in[r][:, rz_cols], start=True, stop=False)
                mm(bank(4)[:, rz_cols], ident[0:H, :], wh_in[r][0:H, rz_cols], start=False, stop=True)
                mm(bank(4)[:, n_cols], wmt[r][:, 0:2 * H], wi_in[r][:, n_cols], start=True, stop=True)
                mm(bank(7)[:, 0:3 * H], wmt[r][:, 2 * H:4 * H], wi_in[r], start=True, stop=True)
                for cols in (rz_cols, n_cols):
                    mm(bank(5)[0:3, cols], bm3[r], wi_in[r][:, cols], start=True, stop=False)
                    mm(bank(5)[0:3, cols], ones[0:1, 0:3], bi_in[r][0:1, cols], start=False, stop=cols == n_cols)
                    if cols == rz_cols:
                        mm(bank(5)[0:3, cols], ones[0:1, 0:3], bh_in[r][0:1, cols], start=False, stop=True)
                mm(bank(5)[0:3, 3 * H:4 * H], ones[0:1, 0:3], bh_in[r][0:1, 2 * H:3 * H], start=True, stop=True
                   ).then_inc(wp_ready, 1)
            pe.wait_ge(ptrs_ready, 2)
            mm(bank(3, NS, 1), ptr_f[0:P, 5:6], ident[0:P, 0:P], start=True, stop=True).then_inc(est_t, 1)
            pe.wait_ge(kwin_in, 5 * 16)
            for j in range(5):
                ins = nc.tensor.transpose(bank(j // 4)[:, (j % 4) * P:(j % 4) * P + P], kwin[0:P, j, :], ident[0:P, 0:P])
            ins.then_inc(win_t, 1)
            pe.wait_ge(ewin_ready, 1)
            for c in range(SC):
                ins = nc.tensor.transpose(bank(2)[:, c * NS:(c + 1) * NS],
                                          ewin_f[0:P, :].rearrange("p (e c) -> p e c", c=SC)[:, :, c], ident[0:P, 0:P])
            ins.then_inc(win_t, 1)
            pe.wait_ge(stats_ready, 1)
            mm(bank(3, 5, 1), ones[:, 0:1], stats, start=True, stop=True).then_inc(stats_sum, 1)

            def adjacency(it, i, ng):
                first, size = BATCHES[i]
                m = min(size, ng - first)
                if m <= 0:
                    return
                pe.wait_ge(one_ready, it * 12 + (2 * i + 2))
                for g in range(first, first + m):
                    u, k = g // 4, g % 4
                    if k == 0:
                        pe.wait_ge(unit_free, it * SU + (5 + (u - 4 if u > 4 else u - 2 if u < 3 else u - 7)))
                    ins = mm(bank(UBANK[u % 5])[:, k * P:k * P + P], one_lo[i % 3][:, g - first, :],
                             one_hi[i % 3][:, g - first, 0:P], start=True, stop=True)
                    if k == 3 or g == ng - 1:
                        ins.then_inc(unit_ready, 1)

            def edge_features(it, k):
                pe.wait_ge(onee_ready, it * 2 + (k // 5 + 1))
                for s in range(k, k + 5):
                    pe.wait_ge(e_in[s], it * 16 + 16)
                    for c in range(SC):
                        ins = mm(PS[H:128, 5, s * SD:(s + 1) * SD], ering[:, s, c, :], one_e[:, s, c, :],
                                 start=(c == 0), stop=(c == SC - 1))
                    ins.then_inc(e_used, 1)

            def gcn_sweep(i, w):
                for s in range(NB):
                    ins = mm(bank(7, w), xparts[0:P, s, :], A3[0:P, s, bass.ds(i * STEP, w)],
                             start=(s == 0), stop=(s == NB - 1))
                ins.then_inc(gsum_ready, 1)

            def gcn_dense(i, nb):
                pe.wait_ge(gsum_copied, i + 1)
                mm(bank(4, nb * P, H), w0t[:, :], gsum[:, 0:nb * P], start=True, stop=True).then_inc(gcn_ready, 1)

            def degrees(it, nb, prev):
                if prev:
                    pe.wait_ge(gcn_used, it)
                for b in range(nb):
                    for c in range(SC):
                        ins = mm(bank(4)[0:P, STEP + b:STEP + b + 1], one_eb[:, c, b * P:(b + 1) * P, 1],
                                 onesb[:, 0:1], start=(c == 0), stop=(c == SC - 1))
                ins.then_inc(esum_ready, 1)

            def build_step(it, ng, ns, prev):
                adjacency(it, 0, ng)
                adjacency(it, 1, ng)
                if prev:
                    pe.wait_ge(unit_free, it * SU + 5)
                    gcn_sweep(it - 1, STEP)
                pe.wait_ge(esum_free, it + 1)
                edge_features(it, 0)
                adjacency(it, 2, ng)
                if prev:
                    gcn_dense(it - 1, 2)
                adjacency(it, 3, ng)
                if ns > 5:
                    edge_features(it, 5)
                adjacency(it, 4, ng)
                adjacency(it, 5, ng)
                degrees(it, ns // 5, prev)

            def sweep(S, t, first, last):
                w = len(blocks_of(t)) * P
                if first == 0 and S >= 2:
                    pe.wait_ge(agg_ready, S - 1)
                for s in range(first, last):
                    if t == 0 and s % 4 == 0:
                        pe.wait_ge(h_ready, S + s // 4 + 1)
                        pe.wait_ge(rest_used, S + s // 4 + 1)
                    ins = mm(bank(S % 2, w), parts[S // NT][0:P, s, :], A3[0:P, s, TILE * t:TILE * t + w],
                             start=(s == 0), stop=(s == NB - 1))
                if last == NB:
                    ins.then_inc(sweep_ready, 1)

            def gcn_back(t):
                if t >= 2:
                    pe.wait_ge(gback_used, t - 1)
                pe.wait_ge(gcn_used, ITS if t < NT - 1 else ITS + 1)
                for i, b in enumerate(blocks_of(t)):
                    ins = nc.tensor.transpose(bank(2 + t % 2)[0:P, i * H:(i + 1) * H], HE[0:H, b * P:(b + 1) * P],
                                              ident[0:H, 0:H])
                ins.then_inc(gback_ready, 1)

            def spread(t):
                w = len(blocks_of(t)) * P
                pe.wait_ge(rdiag_ready, t + 1)
                if t:
                    pe.wait_ge(rdeg_ready, t)
                mm(bank(7, w), ones[0:P, :], rdiag[0:P, 0:w // P, :].rearrange("p b c -> p (b c)"),
                   start=True, stop=True).then_inc(spread_ready, 1)

            def dense(S, t, r, gen):
                if S >= 2:
                    pe.wait_ge(gates_free, S - 1)
                pe.wait_ge(agg_ready, S + 1)
                if r >= 0:
                    pe.wait_ge(he_ready, NT * r + t + 1)
                if r == 0 and not gen:
                    pe.wait_ge(emean_ready, t + 1)
                for i, b in enumerate(blocks_of(t)):
                    mean = agg[S % 2][:, i * P:(i + 1) * P]
                    own = HE[:, b * P:(b + 1) * P]
                    if r < 0:
                        ins = mm(PS[0:P, 2 + 2 * (S % 2), i * H:(i + 1) * H], mean, w0t[:, :], start=True, stop=True)
                        continue
                    at = 2 + 2 * (S % 2) + i // 2
                    lo = (i % 2) * 4 * H
                    mm(PS[0:P, at, lo:lo + 4 * H], own, w_he[r][:, :], start=True, stop=False)
                    mm(PS[0:P, at, lo:lo + 3 * H], mean, w_ag[r][:, :], start=False, stop=False)
                    if gen:
                        mm(PS[0:P, at, lo:lo + 4 * H], hneg[0:H + 1, b * P:(b + 1) * P], w_gen[r][0:H + 1, :],
                           start=False, stop=False)
                    ins = mm(PS[0:P, at, lo:lo + 4 * H], onesb[0:3, 0:P], bias3[r][0:3, :], start=False, stop=True)
                ins.then_inc(gates_ready, 1)

            def transposed(k, t):
                T, h = NT * k + t, (X0, H1)[k]
                pe.wait_ge(h_ready, T + 1)
                if T >= 1:
                    pe.wait_ge(he_ready, T)
                for i, b in enumerate(blocks_of(t)):
                    ins = nc.tensor.transpose(bank(6, 512, H)[:, i * P:(i + 1) * P], h[0:P, b, :], ident[0:P, 0:P])
                ins.then_inc(ht_ready, 1)

            def rounds(gen):
                if gen:
                    for rnd in range(3):
                        general_pass(2 + rnd)
                        for t in range(NT):
                            dense(NT * rnd + t, t, rnd - 1, gen)
                            if rnd < 2:
                                transposed(rnd, t)
                    return
                gcn_back(0)
                gcn_back(1)
                gcn_sweep(ITS, P)
                gcn_dense(ITS, 1)
                for t in range(NT):
                    transposed(0, t)
                    if t + 2 < NT:
                        gcn_back(t + 2)
                    for S in range(2):
                        sweep(S, S, 4 * t, min(4 * t + 4, NB))
                    if t == 4:
                        spread(0)
                for S in range(1, 2 * NT):
                    r, t = S // NT, S % NT
                    if S > 1:
                        sweep(S, t, 0, 10)
                    if 2 <= S < NT + 2:
                        transposed(1, S - 2)
                    if S < NT:
                        spread(S)
                    dense(S - 1, (S - 1) % NT, (S - 1) // NT, gen)
                    if S > 1:
                        sweep(S, t, 10, NB)
                dense(2 * NT - 1, NT - 1, 1, gen)

            def usual():
                pe.sem_inc(unit_ready, UCREDIT)
                pe.sem_inc(esum_ready, 1)
                build_step(0, SG, SS, False)
                pe.wait_ge(parts_ready, 1)
                with pe.Fori(1, ITS) as it:
                    build_step(it, SG, SS, True)
                build_step(ITS, LG, LS, True)
                pe.wait_ge(unit_free, 5 + SU * ITS + LU)
                pe.wait_ge(esum_free, ITS + 2)
                rounds(False)

            def general_pass(q):
                if q:
                    pe.wait_ge(sums_ready, q)
                if q > 2:
                    pe.wait_ge(he_ready, NT * (q - 2))
                    pe.wait_ge(gates_free, NT * (q - 2))
                    pe.wait_ge(neg_ready, 2 + q - 2)
                if q == 0:
                    pe.wait_ge(pass_zeroed, 2)
                tiles = [(t, len(blocks_of(t)) * P) for t in range(NT)]
                for t, w in tiles:
                    mm(bank(t, w), zero_st[0:P, :], iota_n[0:P, TILE * t:TILE * t + w], start=True, stop=False)
                with pe.Fori(0, EC) as c:
                    pe.wait_ge(gone_ready, c + (q * EC + 1))
                    if q == 1:
                        pe.wait_ge(estage_in, c * 16 + 16)
                    if q >= 2:
                        pe.wait_ge(stage_in, c * 16 + ((q - 2) * EC + 1) * 16)
                    for t, w in tiles:
                        ins = mm(bank(t, w), stage[0:P, :], one_n[0:P, TILE * t:TILE * t + w], start=False, stop=False)
                    ins.then_inc(gused, 1)
                for t, w in tiles:
                    ins = mm(bank(t, w), zero_st[0:P, :], iota_n[0:P, TILE * t:TILE * t + w], start=False, stop=True)
                ins.then_inc(pass_done, 1)

            def general():
                pe.wait_ge(gen_c, 2)
                for r in range(2):
                    mm(bank(r, 3 * H, H + 1), wg_l[r], wi_in[r], start=True, stop=True).then_inc(gen_c, 1)
                pe.wait_ge(neg_ready, 2)
                pe.wait_ge(gz_ready, 1)
                pe.sem_inc(gused, 1)
                general_pass(0)
                general_pass(1)
                rounds(True)

            pe.wait_ge(w_done, 3)
            pe.wait_ge(bias_done, 2)
            pe.wait_ge(flag_ready, 1)
            bad_inputs = pe.value_load(flag[0:1, 0:1], min_val=0, max_val=5)
            with pe.If(bad_inputs == 0):
                usual()
            with pe.Else():
                general()


_INS = ["x", "src", "dst", "edge_attr_64", "L0_gnn_W", "L1_gnn_W_msg", "L1_gnn_b_msg", "L1_gnn_W_ih", "L1_gnn_W_hh",
        "L1_gnn_b_ih", "L1_gnn_b_hh"]


def kernel(**inputs):
    import numpy as np
    import concourse.bacc as bacc
    from concourse.bass_utils import run_bass_kernel_spmd

    nc = bacc.Bacc("TRN2", target_bir_lowering=False, num_devices=1, dynamic_dma_scratch_size=4096)
    arrays, args = {}, []
    for name in _INS:
        a = np.ascontiguousarray(inputs[name])
        arrays[f"in_{name}"] = a
        args.append(nc.dram_tensor(f"in_{name}", a.shape, mybir.dt.from_np(a.dtype), kind="ExternalInput").ap())
    out = nc.dram_tensor("out_0", (N, H), mybir.dt.float32, kind="ExternalOutput").ap()
    build(nc, *args, out)
    r = run_bass_kernel_spmd(nc, [arrays], core_ids=[0])
    return r.results[0]["out_0"]
```

```python
from contextlib import ExitStack

import concourse.bass as bass
from concourse import mybir

N, H, E = 3125, 64, 53125
P = 125
NB = N // P
EC = E // P
GD, WIN = 5, 128
NG = N // GD
SD, SC = 25, 4
NS = N // SD
SWIN = SC * 128
XMAX2 = float(2 ** 30)
LO = 2048.0
EPS = 1e-5
TILE = 4 * P
NT = 7
STEP = 2 * P
ITS = N // STEP
SG, SS, SU = STEP // GD, STEP // SD, 13
LG, LS, LU = SG // 2, SS // 2, 7
BATCHES = tuple((8 * i, 8 if i < 5 else 10) for i in range(6))
UCREDIT = 6
BR = 35
PARTS = ((0, 16), (16, 24), (24, NB))
SS_SP = 8
POOL_Y = 22
UBANK = (0, 1, 2, 3, 6)
KW = 126


def blocks_of(t):
    return range(4 * t, min(4 * t + 4, NB))


class Chain:

    def __init__(self, eng, sem):
        self.eng, self.sem, self.n = eng, sem, 0

    def add(self, ins):
        self.n += 1
        ins.then_inc(self.sem, 1)

    def wait(self):
        self.eng.wait_ge(self.sem, self.n)

    def done(self, ins):
        self.add(ins)
        self.wait()


def build(nc, x, src, dst, e, w0, w_msg, b_msg, w_ih, w_hh, b_ih, b_hh, out):
    f32, f16, bf16, i32 = mybir.dt.float32, mybir.dt.float16, mybir.dt.bfloat16, mybir.dt.int32
    ALU, ACT = mybir.AluOpType, mybir.ActivationFunctionType
    ctx = ExitStack()
    with ctx:
        def sb(name, shape, dt=f32):
            return ctx.enter_context(nc.sbuf_tensor(name, shape, dt))

        def sem(name):
            return ctx.enter_context(nc.semaphore(name))

        big = sb("big", [128, (NB * N + 1) // 2])
        HE = sb("HE", [128, N])
        rdeg = sb("rdeg", [128, N])
        mv = sb("mv", [128, NB, 2])
        rstd = sb("rstd", [128, NB])
        rnode = sb("rnode", [128, NB])
        X0 = sb("X0", [128, NB, H])
        work = sb("work", [128, 7630])
        ident = sb("ident", [128, 128])
        ones = sb("ones", [128, 128])
        onesb = sb("onesb", [128, 128], bf16)
        loscale = sb("loscale", [128, 1])
        eps_col = sb("eps_col", [128, 1])
        w0t = sb("w0t", [128, H])
        w_he = [sb(f"w_he{r}", [128, 4 * H]) for r in range(2)]
        w_ag = [sb(f"w_ag{r}", [128, 3 * H]) for r in range(2)]
        bias3 = sb("bias3", [BR, 4 * H], bf16)
        flag = sb("flag", [1, 1], i32)
        A3 = big[:, :].bitcast(f16)[:, 0:NB * N].rearrange("p (s d) -> p s d", s=NB)

        def carve(base):
            at = [0]

            def take(n, dt=f32):
                words = n if dt in (f32, i32) else (n + 1) // 2
                piece = base[:, at[0]:at[0] + words]
                at[0] += words
                assert at[0] <= base.shape[1], at[0]
                return piece if dt == f32 else piece.bitcast(dt)[:, 0:n]
            return take

        take = carve(work)
        iota_k = take(128, bf16)
        iota_d = take(SD)
        lo2 = take(2 * NG, bf16).rearrange("p (g t) -> p g t", t=2)
        hi2 = take(2 * NG, bf16).rearrange("p (g t) -> p g t", t=2)
        ecode = take(SC * NS).rearrange("p (s c) -> p s c", c=SC)
        more = carve(rdeg)
        one_lo = [more(m * 128, bf16).rearrange("p (g k) -> p g k", g=m) for m in (8, 8, 10)]
        one_hi = [t(m * KW, bf16).rearrange("p (g k) -> p g k", g=m) for t, m in ((more, 8), (more, 8), (take, 10))]
        one_e_flat = take(SS * SC * SD)
        one_e = one_e_flat.rearrange("p (c s d) -> p s c d", s=SS, c=SC)
        xparts = take(NB * 2 * H, f16).rearrange("p (b f) -> p b f", b=NB)
        ering = take(SS * SC * H).rearrange("p (s c f) -> p s c f", s=SS, c=SC)
        gsum = more(STEP)
        estart_i = more(NS, i32)
        take = carve(work)
        parts = [take(NB * 2 * H, f16).rearrange("p (b f) -> p b f", b=NB) for _ in range(2)]
        H1 = take(NB * H).rearrange("p (b f) -> p b f", b=NB)
        agg = [take(TILE) for _ in range(2)]
        rz = take(4 * 2 * H).rearrange("p (b f) -> p b f", b=4)
        gout = [rz.rearrange("p b f -> p (b f)")[:, k * 4 * H:(k + 1) * 4 * H].rearrange("p (b f) -> p b f", b=4)
                for k in range(2)]
        cand = take(4 * H).rearrange("p (b f) -> p b f", b=4)
        rest = take(4 * H).rearrange("p (b f) -> p b f", b=4)
        bst = take(6 * 4).rearrange("p (b s) -> p b s", b=4)
        rdiag = take(TILE).rearrange("p (b c) -> p b c", c=P)
        take = carve(big)
        dst_i = take(EC + 1, i32)
        src_i = take(EC, i32)
        dst_f, src_f = take(EC + 1), take(EC)
        q5, hi_f, tmp_f, key = take(EC), take(EC), take(EC), take(EC)
        last_start = take(6)
        thr = take(6)
        gbase = take(NG)
        sbase = take(NS)
        diag = take(128)
        cnt_row, row_f, ptr_f = take(6), take(6), take(6)
        row_i, ptr_i = take(6, i32), take(6, i32)
        found_i = take(6 * EC, i32).rearrange("p (j c) -> p j c", j=6)
        found_f = take(6 * EC).rearrange("p (j c) -> p j c", j=6)
        kwin = take(5 * WIN).rearrange("p (j c) -> p j c", j=5)
        ewin_i = take(SWIN, i32)
        ewin_f = take(SWIN)
        key_i, lo_i, hi_i = take(NG, i32), take(NG, i32), take(NG, i32)
        hi_c, ok_g = take(NG), take(NG)
        ok_e = take(SC * NS).rearrange("p (s c) -> p s c", c=SC)
        xsq = take(NB * H).rearrange("p (b f) -> p b f", b=NB)
        same, step1 = take(EC), take(EC)
        stats, bad, bad1 = take(5), take(5), take(1)
        w0_in = take(2 * H)
        wm_in = [take(3 * 2 * H).rearrange("p (c k) -> p c k", c=3) for _ in range(2)]
        wi_in = [take(3 * H) for _ in range(2)]
        wh_in = [take(3 * H) for _ in range(2)]
        bm_in = [take(1) for _ in range(2)]
        bi_in, bh_in = [take(3 * H) for _ in range(2)], [take(3 * H) for _ in range(2)]
        wmt = [take(4 * H) for _ in range(2)]
        bm3 = [take(3) for _ in range(2)]
        bias_f = take(4 * H)
        part_of = take(3)
        bpart = [take(4 * H, bf16) for _ in range(3)]
        bsel = take(4 * H)
        iota_n = take(N)
        one_n = take(N)
        sums = take(N)
        stage = take(2 * H)
        zero_st = take(2 * H)
        idx_now = take(1, i32)
        hneg = take(N)
        w_gen = [take(4 * H) for _ in range(2)]
        wg_l = [take(H + 1) for _ in range(2)]
        maskm1 = take(N)

        PS = ctx.enter_context(nc.psum_tensor("PS", [128, 8, 512], f32))

        def bank(b, cols=512, rows=128, n=1):
            return PS[0:rows, b, 0:cols] if n == 1 else PS[0:rows, b:b + n, 0:cols]

        def back_bank(t):
            return bank((2, 3, 5, 2)[t // 2])[:, (t % 2) * 4 * H:(t % 2 + 1) * 4 * H]

        one_eb = one_e_flat.bitcast(bf16).rearrange("p (c n t) -> p c n t", c=SC, t=2)
        W_LOADS = 16 * (2 + 2 * 6)
        key_dram = nc.dram_tensor("key_scratch", [E], f32).ap()
        h_dram = nc.dram_tensor("h_scratch", [N, H], f32).ap()
        out3 = out.rearrange("(b p) f -> p b f", p=P)
        h_dram3 = h_dram.rearrange("(b p) f -> p b f", p=P)

        dst_in, src_in, x_in, w_in = sem("dst_in"), sem("src_in"), sem("x_in"), sem("w_in")
        consts = sem("consts")
        first_diag, first_row = sem("first_diag"), sem("first_row")
        rows_ready, found = sem("rows_ready"), [sem(f"found{k}") for k in range(3)]
        key_ready, key_out = sem("key_ready"), sem("key_out")
        ptrs_ready, kwin_in, ewin_in = sem("ptrs_ready"), sem("kwin_in"), sem("ewin_in")
        ewin_ready, win_t, est_t = sem("ewin_ready"), sem("win_t"), sem("est_t")
        stats_ready, stats_sum, flag_ready = sem("stats_ready"), sem("stats_sum"), sem("flag_ready")
        wt_ready, wt_copied, wp_ready, w_done = sem("wt_ready"), sem("wt_copied"), sem("wp_ready"), sem("w_done")
        bias_ready, bias_c, bias_done = sem("bias_ready"), sem("bias_c"), sem("bias_done")
        codes_ready, codes_twice = sem("codes_ready"), sem("codes_twice")
        dve_c, pool_c = sem("dve_c"), sem("pool_c")
        one_ready = sem("one_ready")
        onee_ready = sem("onee_ready")
        unit_ready, unit_free = sem("unit_ready"), sem("unit_free")
        esum_ready, esum_free = sem("esum_ready"), sem("esum_free")
        e_in = [sem(f"e_in{i}") for i in range(SS)]
        e_used = sem("e_used")
        estart_ready = sem("estart_ready")
        parts_ready = sem("parts_ready")
        sweep_ready, agg_ready = sem("sweep_ready"), sem("agg_ready")
        gates_ready, gates_free = sem("gates_ready"), sem("gates_free")
        var_ready, std_ready = sem("var_ready"), sem("std_ready")
        rz_ready, tanh_ready = sem("rz_ready"), sem("tanh_ready")
        h_ready, rest_ready, rest_used = sem("h_ready"), sem("rest_ready"), sem("rest_used")
        ht_ready, he_ready = sem("ht_ready"), sem("he_ready")
        xhigh_ready, xrest_ready, x_whole = sem("xhigh_ready"), sem("xrest_ready"), sem("x_whole")
        rdiag_ready, gvar_ready, gstd_ready = sem("rdiag_ready"), sem("gvar_ready"), sem("gstd_ready")
        gsum_ready, gsum_copied, gcn_ready, gcn_used = sem("gsum_ready"), sem("gsum_copied"), sem("gcn_ready"), sem("gcn_used")
        gback_ready, gscaled, gadded = sem("gback_ready"), sem("gscaled"), sem("gadded")
        rn_ready, normed = sem("rn_ready"), sem("normed")
        xsq_ready = sem("xsq_ready")
        spread_ready, rdeg_ready, emean_ready = sem("spread_ready"), sem("rdeg_ready"), sem("emean_ready")
        idx_ok, estage_in = sem("idx_ok"), sem("estage_in")
        cand_used, w0t_ready = sem("cand_used"), sem("w0t_ready")
        y_ready, out_done = sem("y_ready"), sem("out_done")
        rstd_ready, y_pool = sem("rstd_ready"), sem("y_pool")
        gen_c, stage_in, gone_ready, gused = sem("gen_c"), sem("stage_in"), sem("gone_ready"), sem("gused")
        pass_zeroed, pass_done, sums_ready = sem("pass_zeroed"), sem("pass_done"), sem("sums_ready")
        gz_ready, hstore, idx_set, neg_ready = sem("gz_ready"), sem("hstore"), sem("idx_set"), sem("neg_ready")

        block = ctx.enter_context(nc.Block())

        @block.sync
        def _(sp):
            sp.dma_start(dst_i[0:P, 0:EC], dst.rearrange("(p c) -> p c", c=EC)).then_inc(dst_in, 16)
            sp.wait_ge(consts, 1)
            sp.dma_start(dst_i[0:P - 1, EC:EC + 1], dst[EC:E].rearrange("(p c) -> p c", c=EC)[:, 0:1],
                         allow_slow_non_contiguous=True).then_inc(dst_in, 16)
            sp.dma_start(src_i[0:P, :], src.rearrange("(p c) -> p c", c=EC)).then_inc(src_in, 16)
            sp.dma_start(X0[0:P, :, :], x.rearrange("(b p) f -> p b f", p=P)).then_inc(x_in, 16)
            sp.wait_ge(key_ready, 1)
            sp.dma_start(key_dram.rearrange("(p c) -> p c", c=EC), key[0:P, :]).then_inc(key_out, 16)

            def load_windows(it, first, end, wait):
                for k in range(first, end, 4):
                    here = range(k, min(k + 4, end))
                    _, starts = nc.values_load_multi_w_load_instructions(
                        estart_i[0:1, bass.ds(it * SS + k, len(here))], engines=[mybir.EngineType.SP],
                        min_val=0, max_val=E - SWIN)
                    for s, at in zip(here, starts):
                        if wait:
                            sp.wait_ge(e_used, it * SS + (s + 1 - SS))
                        sp.dma_start(ering[:, s, :, :],
                                     e[bass.ds(at, SWIN), :].rearrange("(p c) f -> p c f", c=SC)
                                     ).then_inc(e_in[s], 16)

            def usual():
                with sp.Fori(1, ITS) as it:
                    load_windows(it, 0, SS_SP, True)
                load_windows(ITS, 0, LS, True)

            def general():
                for s in range(SS_SP):
                    sp.wait_ge(e_in[s], 16)
                sp.wait_ge(gz_ready, 2)
                e3 = e.rearrange("(p c) f -> p c f", c=EC)
                with sp.Fori(0, EC) as c:
                    sp.wait_ge(gused, c + (EC + 1))
                    sp.dma_start(stage[0:P, H:2 * H], e3[:, bass.ds(c, 1), :].rearrange("p c f -> p (c f)")
                                 ).then_inc(estage_in, 16)
                for r, hbuf in ((1, X0), (2, H1)):
                    sp.wait_ge(h_ready, NT * r)
                    sp.dma_start(h_dram3, hbuf[0:P, :, :]).then_inc(hstore, 16)
                    sp.wait_ge(hstore, 16 * r)

            sp.wait_ge(estart_ready, 1)
            load_windows(0, 0, SS_SP, False)
            sp.wait_ge(flag_ready, 1)
            bad_inputs = sp.value_load(flag[0:1, 0:1], min_val=0, max_val=5)
            with sp.If(bad_inputs == 0):
                usual()
            with sp.Else():
                general()
            for k, (first, end) in enumerate(PARTS):
                sp.wait_ge(y_ready, k + 1)
                if k == 1:
                    sp.wait_ge(y_pool, end - POOL_Y)
                sp.dma_start(out3[:, first:end, :], H1[0:P, first:end, :]).then_inc(out_done, 16)
            sp.wait_ge(out_done, 3 * 16)

        @block.gpsimd
        def _(pool):
            pool.memset(dst_i[:, EC:EC + 1], N).then_inc(consts, 1)
            pool.memset(ones[:, :], 1.0).then_inc(consts, 1)
            pool.memset(onesb[:, :], 1.0).then_inc(consts, 1)
            pool.memset(ident[:, :], 0.0).then_inc(pool_c, 1)
            pool.wait_ge(pool_c, 1)
            pool.affine_select(out=ident[:, :], in_=ident[:, :], compare_op=ALU.not_equal, fill=1.0, base=0,
                               pattern=[[-1, 128]], channel_multiplier=1).then_inc(consts, 1)
            pool.iota(thr[:, 0:5], pattern=[[GD * P, 5]], base=0, channel_multiplier=GD,
                      allow_small_or_imprecise_dtypes=True).then_inc(consts, 1)
            pool.iota(thr[:, 5:6], pattern=[[0, 1]], base=0, channel_multiplier=SD,
                      allow_small_or_imprecise_dtypes=True).then_inc(consts, 1)
            pool.memset(bias_f, 0.0).then_inc(consts, 1)
            pool.memset(last_start[:, 0:5], float(E - WIN)).then_inc(consts, 1)
            pool.memset(last_start[:, 5:6], float(E - SWIN)).then_inc(consts, 1)
            pool.memset(stats, 0.0).then_inc(consts, 1)
            pool.memset(loscale[0:H, :], 1.0).then_inc(consts, 1)
            pool.wait_ge(consts, 11)
            pool.memset(loscale[H:128, :], 1.0 / LO).then_inc(consts, 1)
            for r in range(2):
                pool.memset(w_he[r][H:128, 3 * H:4 * H], 0.0).then_inc(consts, 1)
            pool.wait_ge(consts, 14)
            pool.memset(eps_col[:, :], EPS).then_inc(consts, 1)
            pool.iota(iota_k, pattern=[[1, 128]], base=0, channel_multiplier=0,
                      allow_small_or_imprecise_dtypes=True).then_inc(consts, 1)
            pool.iota(iota_d, pattern=[[1, SD]], base=0, channel_multiplier=0,
                      allow_small_or_imprecise_dtypes=True).then_inc(consts, 1)
            for two in one_lo:
                pool.memset(two[:, :, KW:128], 0.0).then_inc(consts, 1)
            for j, total in enumerate((E, E, N, E - N, N * H)):
                pool.memset(bad[0:1, j:j + 1], float(total)).then_inc(consts, 1)
            pool.wait_ge(rows_ready, 1)
            dst_rows = dst.rearrange("(r c) -> r c", c=EC)
            for j in range(6):
                pool.indirect_dma_start(out=found_i[0:P, j, :], out_offset=None, in_=dst_rows,
                                        in_offset=bass.IndirectOffsetOnAxis(ap=row_i[0:P, j:j + 1], axis=0)
                                        ).then_inc(found[j // 2], 16)
            pool.wait_ge(key_out, 16)
            key_rows = key_dram.rearrange("(n o) -> n o", o=1)
            for j in range(5):
                if j % 2 == 0:
                    pool.wait_ge(ptrs_ready, j // 2 + 1)
                pool.indirect_dma_start(out=kwin[0:P, j, :], out_offset=None, in_=key_rows,
                                        in_offset=bass.IndirectOffsetOnAxis(ap=ptr_i[0:P, j:j + 1], axis=0)
                                        ).then_inc(kwin_in, 16)
            pool.indirect_dma_start(out=ewin_i[0:P, :], out_offset=None, in_=dst.rearrange("(n o) -> n o", o=1),
                                    in_offset=bass.IndirectOffsetOnAxis(ap=ptr_i[0:P, 5:6], axis=0)
                                    ).then_inc(ewin_in, 16)
            pool.iota(gbase, pattern=[[P, NG]], base=0, channel_multiplier=0,
                      allow_small_or_imprecise_dtypes=True).then_inc(consts, 1)
            pool.iota(sbase, pattern=[[SD, NS]], base=0, channel_multiplier=0,
                      allow_small_or_imprecise_dtypes=True).then_inc(consts, 1)
            bc = Chain(pool, bias_c)
            tt = nc.gpsimd.tensor_tensor
            bc.done(tt(part_of[0:BR, :], ident[0:BR, 0:3], ident[0:BR, 32:BR], ALU.add))
            pool.wait_ge(bias_ready, 2)
            bf = bias_f[0:BR, :]
            for k in range(3):
                bc.done(pool.tensor_copy(bpart[k][0:BR, :], bf))
                if k < 2:
                    bc.done(tt(bf, bf, bpart[k][0:BR, :], ALU.subtract))
            for k in range(3):
                to = bf if k else bsel[0:BR, :]
                bc.done(tt(to, bpart[k][0:BR, :], part_of[0:BR, k:k + 1].to_broadcast([BR, 4 * H]), ALU.mult))
                if k:
                    bc.done(tt(bsel[0:BR, :], bsel[0:BR, :], bf, ALU.add))
            pool.tensor_copy(bias3[0:BR, :], bsel[0:BR, :]).then_inc(bias_done, 1)
            pool.wait_ge(bias_done, 1)

            def load_windows(it, first, end, wait):
                for k in range(first, end, 4):
                    here = range(k, min(k + 4, end))
                    _, starts = nc.values_load_multi_w_load_instructions(
                        estart_i[0:1, bass.ds(it * SS + k, len(here))], engines=[mybir.EngineType.Pool],
                        min_val=0, max_val=E - SWIN)
                    for s, at in zip(here, starts):
                        if wait:
                            pool.wait_ge(e_used, it * SS + (s + 1 - SS))
                        pool.dma_start(ering[:, s, :, :],
                                     e[bass.ds(at, SWIN), :].rearrange("(p c) f -> p c f", c=SC)
                                     ).then_inc(e_in[s], 16)

            def general():
                pool.iota(iota_n, pattern=[[1, N]], base=0, channel_multiplier=0,
                          allow_small_or_imprecise_dtypes=True).then_inc(gz_ready, 1)
                pool.memset(zero_st, 0.0).then_inc(pass_zeroed, 1)
                pool.memset(stage, 1.0).then_inc(pass_zeroed, 1)
                pool.wait_ge(gused, EC + 1)
                pool.memset(stage[:, 0:H], 0.0).then_inc(gz_ready, 1)
                pool.wait_ge(gused, 2 * EC + 1)
                pool.memset(stage[:, H:2 * H], 0.0).then_inc(gz_ready, 1)
                for r in range(3):
                    if r:
                        pool.wait_ge(hstore, 16 * r)
                    table = x if r == 0 else h_dram
                    with pool.Fori(0, EC) as c:
                        pool.wait_ge(gused, c + ((2 + r) * EC + 1))
                        pool.tensor_copy(idx_now[0:P, :], src_i[0:P, bass.ds(c, 1)]).then_inc(idx_set, 1)
                        pool.wait_ge(idx_set, c + (r * EC + 1))
                        pool.sem_inc(idx_ok, 1)
                        pool.indirect_dma_start(out=stage[0:P, 0:H], out_offset=None, in_=table,
                                                in_offset=bass.IndirectOffsetOnAxis(ap=idx_now[0:P, 0:1], axis=0)
                                                ).then_inc(stage_in, 16)

            pool.wait_ge(flag_ready, 1)
            bad_inputs = pool.value_load(flag[0:1, 0:1], min_val=0, max_val=5)
            with pool.If(bad_inputs == 0):
                pool.wait_ge(xhigh_ready, 1)
                nc.gpsimd.tensor_tensor(X0[0:P, :, :], X0[0:P, :, :], xparts[0:P, :, 0:H], ALU.subtract
                                        ).then_inc(xrest_ready, 1)
                load_windows(0, SS_SP, SS, False)
                pool.wait_ge(parts_ready, 1)
                nc.gpsimd.tensor_tensor(X0[0:P, :, :], X0[0:P, :, :], xparts[0:P, :, 0:H], ALU.add
                                        ).then_inc(x_whole, 1)
                pool.wait_ge(x_whole, 1)
                with pool.Fori(1, ITS) as it:
                    load_windows(it, SS_SP, SS, True)
                for t in range(NT):
                    blks = blocks_of(t)
                    sl = slice(blks[0], blks[-1] + 1)
                    pool.wait_ge(gscaled, t + 1)
                    nc.gpsimd.tensor_tensor(X0[0:P, sl, :], X0[0:P, sl, :], gout[t % 2][0:P, 0:len(blks), :], ALU.add
                                            ).then_inc(gadded, 1)
                for t in range(NT):
                    cols = slice(TILE * t, TILE * t + len(blocks_of(t)) * P)
                    pool.wait_ge(rdeg_ready, t + 1)
                    nc.gpsimd.tensor_tensor(HE[H:128, cols], HE[H:128, cols], rdeg[H:128, cols], ALU.mult
                                            ).then_inc(emean_ready, 1)
            with pool.Else():
                general()
            pool.wait_ge(rstd_ready, 2)
            for b in range(POOL_Y, PARTS[1][1]):
                nc.gpsimd.tensor_scalar(H1[0:P, b, :], H1[0:P, b, :], mv[0:P, b, 0:1], rstd[0:P, b:b + 1],
                                        ALU.subtract, ALU.mult).then_inc(y_pool, 1)

        @block.vector
        def _(dve):
            ch = Chain(dve, dve_c)
            v = nc.vector
            MAGIC = 12582912.0

            dve.wait_ge(dst_in, 32)
            ch.done(v.tensor_copy(dst_f[0:P, :], dst_i[0:P, :]))
            dve.wait_ge(consts, 25)
            v.tensor_scalar(diag[0:P, 0:P], ident[0:P, 0:P], dst_f[0:P, 0:1], None, ALU.mult).then_inc(first_diag, 1)
            ch.done(v.tensor_scalar(q5[0:P, :], dst_f[0:P, 0:EC], 0.2, -0.4, ALU.mult, ALU.add))
            ch.done(v.tensor_scalar(q5[0:P, :], q5[0:P, :], MAGIC, -MAGIC, ALU.add, ALU.add))
            dve.wait_ge(first_row, 1)
            for j in range(6):
                ch.add(v.tensor_scalar(found_f[0:P, j, 0:P], bank(0, P, P), thr[0:P, j:j + 1], None, ALU.is_lt,
                                       ALU.add, accum_out=cnt_row[0:P, j:j + 1]))
            ch.wait()
            ch.done(v.tensor_scalar(row_f[0:P, :], cnt_row[0:P, :], -1.0, 0.0, ALU.add, ALU.max))
            v.tensor_copy(row_i[0:P, :], row_f[0:P, :]).then_inc(rows_ready, 1)
            dve.wait_ge(src_in, 16)
            ch.done(v.tensor_copy(src_f[0:P, :], src_i[0:P, :]))
            ch.done(v.tensor_scalar(hi_f[0:P, :], src_f[0:P, :], 1.0 / P, -(P - 1) / 2.0 / P, ALU.mult, ALU.add))
            ch.done(v.tensor_scalar(hi_f[0:P, :], hi_f[0:P, :], MAGIC, -MAGIC, ALU.add, ALU.add))
            ch.done(v.scalar_tensor_tensor(src_f[0:P, :], hi_f[0:P, :], -float(P), src_f[0:P, :], ALU.mult, ALU.add))
            ch.done(v.scalar_tensor_tensor(tmp_f[0:P, :], hi_f[0:P, :], float(GD), dst_f[0:P, 0:EC], ALU.mult, ALU.add))
            ch.done(v.scalar_tensor_tensor(tmp_f[0:P, :], q5[0:P, :], float(NB * GD - GD), tmp_f[0:P, :], ALU.mult, ALU.add))
            v.scalar_tensor_tensor(key[0:P, :], tmp_f[0:P, :], 128.0, src_f[0:P, :], ALU.mult, ALU.add).then_inc(key_ready, 1)
            for k in range(3):
                dve.wait_ge(found[k], 2 * 16)
                cols = slice(2 * k, 2 * k + 2)
                for j in range(2 * k, 2 * k + 2):
                    ch.add(v.tensor_scalar(found_f[0:P, j, :], found_i[0:P, j, :], thr[0:P, j:j + 1], None, ALU.is_lt,
                                           ALU.add, accum_out=cnt_row[0:P, j:j + 1]))
                ch.wait()
                ch.done(v.scalar_tensor_tensor(ptr_f[0:P, cols], row_f[0:P, cols], float(EC), cnt_row[0:P, cols],
                                               ALU.mult, ALU.add))
                ch.done(v.tensor_tensor(ptr_f[0:P, cols], ptr_f[0:P, cols], last_start[0:P, cols], ALU.min))
                v.tensor_copy(ptr_i[0:P, cols], ptr_f[0:P, cols]).then_inc(ptrs_ready, 1)

            ch.done(v.tensor_tensor(same[0:P, :], dst_f[0:P, 1:EC + 1], dst_f[0:P, 0:EC], ALU.subtract))
            ch.done(v.tensor_scalar(step1[0:P, :], same[0:P, :], 1.0, None, ALU.is_equal, ALU.add,
                                    accum_out=stats[0:P, 2:3]))
            ch.done(v.tensor_scalar(step1[0:P, :], same[0:P, :], 0.0, None, ALU.is_equal, ALU.add,
                                    accum_out=stats[0:P, 3:4]))
            dve.wait_ge(xsq_ready, 1)
            ch.done(v.tensor_scalar(xsq[0:P, :, :], xsq[0:P, :, :], XMAX2, None, ALU.is_le, ALU.add,
                                    accum_out=stats[0:P, 4:5]))
            dve.wait_ge(est_t, 1)
            v.tensor_copy(estart_i[0:1, :], bank(3, NS, 1)).then_inc(estart_ready, 1)
            dve.wait_ge(ewin_in, 16)
            v.tensor_copy(ewin_f[0:P, :], ewin_i[0:P, :]).then_inc(ewin_ready, 1)

            dve.wait_ge(win_t, 1)
            ch.done(v.tensor_copy(key_i[:, 0:500], bank(0, 500)))
            ch.done(v.tensor_copy(key_i[:, 500:NG], bank(1, NG - 500)))
            dve.wait_ge(consts, 27)
            ch.done(v.tensor_scalar(lo_i, key_i, 127, None, ALU.bitwise_and))
            ch.done(v.tensor_scalar(hi_i, key_i, 7, None, ALU.logical_shift_right))
            dve.sem_inc(codes_ready, 1)
            ch.done(v.tensor_tensor(hi_c, hi_i, gbase, ALU.subtract))
            dve.sem_inc(codes_ready, 1)
            ch.done(v.tensor_scalar(ok_g, hi_c, 0.0, None, ALU.is_ge))
            ch.done(v.scalar_tensor_tensor(ok_g, hi_c, float(NB * GD), ok_g, ALU.is_lt, ALU.mult,
                                           accum_out=stats[:, 0:1]))
            dve.wait_ge(win_t, 2)
            ch.done(v.tensor_tensor(ecode, bank(2, SC * NS).rearrange("p (c s) -> p s c", c=SC),
                                    sbase.unsqueeze(2).to_broadcast([128, NS, SC]), ALU.subtract))
            ch.done(v.tensor_scalar(ok_e, ecode, 0.0, None, ALU.is_ge))
            ch.done(v.scalar_tensor_tensor(ok_e, ecode, float(SD), ok_e, ALU.is_lt, ALU.mult,
                                           accum_out=stats[:, 1:2]))
            dve.sem_inc(stats_ready, 1)
            dve.wait_ge(codes_twice, 2)
            dve.wait_ge(stats_sum, 1)
            ch.done(v.tensor_tensor(bad[0:1, :], bank(3, 5, 1), bad[0:1, :], ALU.not_equal))
            ch.done(v.tensor_reduce(bad1[0:1, :], bad[0:1, :], mybir.AxisListType.X, ALU.add))
            v.tensor_copy(flag[0:1, :], bad1[0:1, :]).then_inc(flag_ready, 1)

            def one_hots(it, i, ng):
                first, size = BATCHES[i]
                m = min(size, ng - first)
                if m <= 0:
                    return
                dve.wait_ge(unit_ready, it * SU + (UCREDIT + (2 * (i - 2) if i > 2 else (-5, -3, 0)[i])))
                for two, codes in ((one_lo[i % 3], lo2), (one_hi[i % 3], hi2)):
                    v.tensor_tensor(
                        two[:, 0:m, 0:KW].rearrange("p g (k t) -> p g k t", t=2),
                        codes[:, bass.ds(it * SG + first, m), :].unsqueeze(2).to_broadcast([128, m, KW // 2, 2]),
                        iota_k[:, 0:KW].rearrange("p (k t) -> p k t", t=2).unsqueeze(1).to_broadcast([128, m, KW // 2, 2]),
                        ALU.is_equal).then_inc(one_ready, 1)

            def one_es(it, ns):
                dve.wait_ge(esum_ready, it + 1)
                for k in range(0, ns, 5):
                    v.tensor_tensor(one_e[:, k:k + 5, :, :],
                                    ecode[:, bass.ds(it * SS + k, 5), :].unsqueeze(3).to_broadcast([128, 5, SC, SD]),
                                    iota_d.unsqueeze(1).unsqueeze(1).to_broadcast([128, 5, SC, SD]),
                                    ALU.is_equal).then_inc(onee_ready, 1)

            def build_step(it, ng, ns):
                for i in range(6):
                    one_hots(it, i, ng)
                    if i == 2:
                        one_es(it, ns)

            def spread(t):
                blks = blocks_of(t)
                if t:
                    dve.wait_ge(spread_ready, t)
                v.tensor_tensor(rdiag[0:P, 0:len(blks), :], ident[0:P, 0:P].unsqueeze(1).to_broadcast([P, len(blks), P]),
                                rnode[0:P, blks[0]:blks[-1] + 1].unsqueeze(2).to_broadcast([P, len(blks), P]),
                                ALU.mult).then_inc(rdiag_ready, 1)

            def mean(S, t, gen):
                if S < NT and not gen:
                    dve.wait_ge(rdeg_ready, t + 1)
                w = len(blocks_of(t)) * P
                if S >= 2:
                    dve.wait_ge(gates_ready, S - 1)
                if gen:
                    from_ = sums[:, TILE * t:TILE * t + w]
                else:
                    dve.wait_ge(sweep_ready, S + 1)
                    from_ = bank(S % 2, w)
                v.tensor_tensor(agg[S % 2][:, 0:w], from_, rdeg[:, TILE * t:TILE * t + w], ALU.mult
                                ).then_inc(agg_ready, 1)

            def moments(y, t):
                for i, b in enumerate(blocks_of(t)):
                    ch.add(v.bn_stats(bst[0:P, i, :], y[0:P, b, :]))
                ch.wait()
                for i, b in enumerate(blocks_of(t)):
                    ch.add(v.bn_aggr(mv[0:P, b, :], bst[0:P, i, :]))
                ch.wait()

            def normalize(y, blks):
                for b in blks:
                    ch.add(v.tensor_scalar(y[0:P, b, :], y[0:P, b, :], mv[0:P, b, 0:1], rstd[0:P, b:b + 1],
                                           ALU.subtract, ALU.mult))
                ch.wait()

            def hand_over(k, h, t, gen):
                T = NT * k + t
                blks = blocks_of(t)
                sl = slice(blks[0], blks[-1] + 1)
                if gen:
                    dve.sem_inc(h_ready, 1)
                    return
                p = parts[k]
                v.tensor_copy(p[0:P, sl, 0:H], h[0:P, sl, :]).then_inc(h_ready, 1)
                dve.wait_ge(h_ready, T + 1)
                if T >= 1:
                    dve.wait_ge(rest_used, T)
                v.tensor_tensor(rest[0:P, 0:len(blks), :], h[0:P, sl, :], p[0:P, sl, 0:H], ALU.subtract
                                ).then_inc(rest_ready, 1)

            def gcn_stats(t):
                sl = slice(blocks_of(t)[0], blocks_of(t)[-1] + 1)
                dve.wait_ge(gadded, t + 1)
                moments(X0, t)
                v.tensor_copy(rstd[0:P, sl], mv[0:P, sl, 1]).then_inc(gvar_ready, 1)

            def gcn_rest(t):
                blks = blocks_of(t)
                sl = slice(blks[0], blks[-1] + 1)
                dve.wait_ge(h_ready, t + 1)
                if t >= 1:
                    dve.wait_ge(rest_used, t)
                v.tensor_tensor(rest[0:P, 0:len(blks), :], X0[0:P, sl, :], parts[0][0:P, sl, 0:H], ALU.subtract
                                ).then_inc(rest_ready, 1)

            def gcn(t):
                blks = blocks_of(t)
                n, sl = len(blks), slice(blks[0], blks[-1] + 1)
                dve.wait_ge(gates_ready, t + 1)
                v.tensor_tensor(X0[0:P, sl, :], X0[0:P, sl, :],
                                bank(2 + 2 * (t % 2), n * H, P).rearrange("p (b f) -> p b f", f=H), ALU.add
                                ).then_inc(gates_free, 1)
                dve.wait_ge(gates_free, t + 1)
                moments(X0, t)
                v.tensor_copy(rstd[0:P, sl], mv[0:P, sl, 1]).then_inc(var_ready, 1)
                dve.wait_ge(std_ready, t + 1)
                ch.done(v.reciprocal(rstd[0:P, sl], rstd[0:P, sl]))
                normalize(X0, blks)
                hand_over(0, X0, t, True)

            def gru(r, t, gen):
                S, G, blks = NT * (r + gen) + t, NT * r + t, blocks_of(t)
                n, sl = len(blks), slice(blks[0], blks[-1] + 1)
                old = X0 if r == 0 else H1
                gates = bank(2 + 2 * (S % 2), 512, P, 2).rearrange("p a (b f) -> p (a b) f", b=2)
                dve.wait_ge(rz_ready, G + 1)
                ch.done(v.tensor_tensor(cand[0:P, 0:n, :], rz[0:P, 0:n, 0:H], gates[:, 0:n, 3 * H:4 * H], ALU.mult))
                v.tensor_tensor(cand[0:P, 0:n, :], cand[0:P, 0:n, :], gates[:, 0:n, 2 * H:3 * H], ALU.add
                                ).then_inc(gates_free, 1)
                if t == NT - 2:
                    mean(S + 1, t + 1, gen)
                dve.wait_ge(tanh_ready, G + 1)
                ch.done(v.tensor_tensor(H1[0:P, sl, :], old[0:P, sl, :], cand[0:P, 0:n, :], ALU.subtract))
                ch.done(v.tensor_tensor(H1[0:P, sl, :], H1[0:P, sl, :], rz[0:P, 0:n, H:2 * H], ALU.mult))
                v.tensor_tensor(H1[0:P, sl, :], H1[0:P, sl, :], cand[0:P, 0:n, :], ALU.add).then_inc(cand_used, 1)
                dve.wait_ge(cand_used, G + 1)
                if r == 1:
                    ch.done(v.tensor_tensor(H1[0:P, sl, :], H1[0:P, sl, :], X0[0:P, sl, :], ALU.add))

            def rounds(gen):
                if gen:
                    for t in range(NT):
                        mean(t, t, gen)
                        gcn(t)
                for r in range(2):
                    if gen:
                        neg_h(r)
                        general_pass(3 + r)
                    mean(NT * (r + gen), 0, gen)
                    for t in range(NT):
                        if r == 0 and t + 1 < NT and not gen:
                            spread(t + 1)
                        gru(r, t, gen)
                        if t + 2 < NT:
                            mean(NT * (r + gen) + t + 1, t + 1, gen)
                        if r == 0:
                            hand_over(1, H1, t, gen)
                            continue
                        moments(H1, t)
                        if t in (3, 5, 6):
                            first, end = PARTS[(3, 5, 6).index(t)]
                            v.tensor_copy(rstd[0:P, first:end], mv[0:P, first:end, 1]).then_inc(var_ready, 1)
                        if t == 4:
                            last_norm(0, gen)
                last_norm(1, gen)
                last_norm(2, gen)

            def last_norm(k, gen):
                first, end = PARTS[k]
                dve.wait_ge(std_ready, k + 1 + (NT if gen else 0))
                v.reciprocal(rstd[0:P, first:end], rstd[0:P, first:end]).then_inc(rstd_ready, 1)
                dve.wait_ge(rstd_ready, k + 1)
                normalize(H1, range(first, POOL_Y if k == 1 else end))
                dve.sem_inc(y_ready, 1)

            def usual():
                with dve.Fori(0, ITS) as it:
                    build_step(it, SG, SS)
                build_step(ITS, LG, LS)
                dve.wait_ge(gcn_used, ITS)
                v.reciprocal(rnode[0:P, 0:NB - 1], rnode[0:P, 0:NB - 1]).then_inc(rn_ready, 1)
                dve.wait_ge(unit_ready, UCREDIT + SU * ITS + LU)
                dve.wait_ge(esum_ready, ITS + 2)
                gcn_stats(0)
                gcn_stats(1)
                for t in range(NT):
                    sl = slice(blocks_of(t)[0], blocks_of(t)[-1] + 1)
                    dve.wait_ge(gstd_ready, t + 1)
                    ch.done(v.reciprocal(rstd[0:P, sl], rstd[0:P, sl]))
                    normalize(X0, blocks_of(t))
                    dve.sem_inc(normed, 1)
                    if t == 3:
                        dve.wait_ge(gcn_used, ITS + 1)
                        v.reciprocal(rnode[0:P, NB - 1:NB], rnode[0:P, NB - 1:NB]).then_inc(rn_ready, 1)
                    if t + 2 < NT:
                        gcn_stats(t + 2)
                    if t >= 1:
                        gcn_rest(t - 1)
                    if t == 4:
                        dve.wait_ge(rn_ready, 2)
                        spread(0)
                gcn_rest(NT - 1)
                rounds(False)

            def general_pass(q):
                with dve.Fori(0, EC) as c:
                    dve.wait_ge(gused, c + (q * EC + 1))
                    v.tensor_scalar(one_n[0:P, :], iota_n[0:P, :], dst_f[0:P, bass.ds(c, 1)], None, ALU.is_equal
                                    ).then_inc(gone_ready, 1)
                dve.wait_ge(pass_done, q + 1)
                for t in range(NT):
                    w = len(blocks_of(t)) * P
                    ch.add(v.tensor_copy(sums[:, TILE * t:TILE * t + w], bank(t, w)))
                ch.wait()
                dve.sem_inc(sums_ready, 1)

            def neg_h(r):
                dve.wait_ge(he_ready, NT * (r + 1))
                ch.done(v.tensor_tensor(hneg[0:H, :], maskm1[0:H, :], HE[0:H, :], ALU.mult))
                v.tensor_copy(hneg[H:H + 1, :], maskm1[H:H + 1, :]).then_inc(neg_ready, 1)

            def general():
                dve.wait_ge(gz_ready, 1)
                for r in range(2):
                    ch.done(v.tensor_copy(wg_l[r][:, 0:H], wmt[r][:, 0:H]))
                    v.tensor_copy(wg_l[r][:, H:H + 1], bm_in[r]).then_inc(gen_c, 1)
                for r in range(2):
                    dve.wait_ge(gen_c, 3 + r)
                    ch.done(v.tensor_copy(w_gen[r][0:H + 1, 0:3 * H], bank(r, 3 * H, H + 1)))
                    v.memset(w_gen[r][0:H + 1, 3 * H:4 * H], 0.0).then_inc(neg_ready, 1)
                general_pass(0)
                for s in range(SS_SP):
                    dve.wait_ge(e_in[s], 16)
                ch.done(v.tensor_scalar(maskm1, sums, 1.0, -1.0, ALU.min, ALU.add))
                ch.done(v.tensor_scalar(sums, sums, 1.0, None, ALU.max))
                ch.done(v.reciprocal(rdeg[:, :], sums))
                general_pass(1)
                ch.done(v.tensor_tensor(HE[H:128, :], sums[H:128, :], rdeg[H:128, :], ALU.mult))
                general_pass(2)
                rounds(True)

            dve.wait_ge(flag_ready, 1)
            bad_inputs = dve.value_load(flag[0:1, 0:1], min_val=0, max_val=5)
            base = ch.n
            with dve.If(bad_inputs == 0):
                usual()
            ch.n = base
            with dve.Else():
                general()

        @block.scalar
        def _(act):
            a = nc.scalar
            for half in range(2):
                act.dma_start(w0_in[0:H, half * H:(half + 1) * H], w0).then_inc(w_in, 16)
            for r in range(2):
                act.dma_start(wm_in[r][0:H, :, :], w_msg[r].rearrange("(c p) k -> p c k", p=H)).then_inc(w_in, 16)
                act.dma_start(wi_in[r], w_ih[r]).then_inc(w_in, 16)
                act.dma_start(wh_in[r][0:H, :], w_hh[r]).then_inc(w_in, 16)
                act.dma_start(bm_in[r], b_msg[r].rearrange("(k o) -> k o", o=1)).then_inc(w_in, 16)
                act.dma_start(bi_in[r][0:1, :], b_ih[r:r + 1, :]).then_inc(w_in, 16)
                act.dma_start(bh_in[r][0:1, :], b_hh[r:r + 1, :]).then_inc(w_in, 16)
            act.wait_ge(x_in, 16)
            act.activation(xsq[0:P, :, :], X0[0:P, :, :], ACT.Square).then_inc(xsq_ready, 1)
            act.wait_ge(w_in, W_LOADS)
            for r in range(2):
                act.activation(bm3[r], bm_in[r].to_broadcast([128, 3]), ACT.Copy)
                act.wait_ge(wt_ready, r + 1)
                act.activation(wmt[r], bank(6 + r, 4 * H), ACT.Copy).then_inc(wt_copied, 1)
            for r in range(2):
                act.wait_ge(wp_ready, r + 1)
                act.activation(bias_f[32 * r:32 * r + 3, :], bank(5)[32 * r:32 * r + 3, 0:4 * H], ACT.Copy).then_inc(bias_ready, 1)
                act.activation(w_he[r][:, 0:3 * H], bank(4, 3 * H), ACT.Copy)
                act.activation(w_he[r][0:H, 3 * H:4 * H], wh_in[r][0:H, 2 * H:3 * H], ACT.Copy)
                act.activation(w_ag[r][:, :], bank(7, 3 * H), ACT.Copy, scale=loscale[:, 0:1]).then_inc(w_done, 1)
            act.wait_ge(w0t_ready, 1)
            act.activation(w0t[:, :], bank(6, H), ACT.Copy, scale=loscale[:, 0:1]).then_inc(w_done, 1)
            act.wait_ge(codes_ready, 1)
            act.activation(lo2, lo_i.unsqueeze(2).to_broadcast([128, NG, 2]), ACT.Copy).then_inc(codes_twice, 1)
            act.wait_ge(codes_ready, 2)
            act.activation(hi2, hi_c.unsqueeze(2).to_broadcast([128, NG, 2]), ACT.Copy).then_inc(codes_twice, 1)

            def unit(it, u, n):
                act.wait_ge(unit_ready, it * SU + (u + 1 + UCREDIT))
                act.activation(
                    A3[:, :, bass.ds(it * STEP + 20 * u, n * GD)].rearrange("p s (g d) -> p s g d", g=n),
                    bank(UBANK[u % 5], n * P).rearrange("p (g s d) -> p s g d", g=n, d=GD), ACT.Copy
                ).then_inc(unit_free, 1)

            def edge_sums(it, ns):
                act.wait_ge(esum_ready, it + 2)
                act.activation(HE[H:128, bass.ds(it * STEP, ns * SD)], PS[H:128, 5, 0:ns * SD], ACT.Copy
                               ).then_inc(esum_free, 1)

            def gcn_sums(i, nb):
                act.wait_ge(gsum_ready, i + 1)
                act.activation(gsum[:, 0:nb * P], bank(7, nb * P), ACT.Copy).then_inc(gsum_copied, 1)

            def gcn_out(i, nb):
                act.wait_ge(gcn_ready, i + 1)
                act.activation(HE[0:H, bass.ds(i * STEP, nb * P)], bank(4, nb * P, H), ACT.Copy)
                act.activation(rnode[0:P, bass.ds(i * 2, nb)], bank(4)[0:P, STEP:STEP + nb], ACT.Copy).then_inc(gcn_used, 1)

            def build_step(it, units, ng, ns, prev):
                for u in range(units):
                    if u == 6 and not prev:
                        act.wait_ge(xrest_ready, 1)
                        act.activation(xparts[0:P, :, H:2 * H], X0[0:P, :, :], ACT.Copy, scale=LO).then_inc(parts_ready, 1)
                    if u == 6 and prev:
                        gcn_sums(it - 1, 2)
                    if u == 9 and prev:
                        gcn_out(it - 1, 2)
                    unit(it, u, min(4, ng - 4 * u))
                if units == 7:
                    gcn_out(it - 1, 2)
                edge_sums(it, ns)

            def hand_over(k, t, gen):
                T, blks = NT * k + t, blocks_of(t)
                n, w, sl = len(blks), len(blks) * P, slice(blks[0], blks[-1] + 1)
                if not gen:
                    act.wait_ge(rest_ready, T + 1)
                    a.activation(parts[k][0:P, sl, H:2 * H], rest[0:P, 0:n, :], ACT.Copy,
                                 scale=LO).then_inc(rest_used, 1)
                act.wait_ge(ht_ready, T + 1)
                a.activation(HE[0:H, TILE * t:TILE * t + w], bank(6, w, H), ACT.Copy).then_inc(he_ready, 1)

            def rounds(gen):
                def spread(t):
                    w = len(blocks_of(t)) * P
                    act.wait_ge(spread_ready, t + 1)
                    a.activation(rdeg[:, TILE * t:TILE * t + w], bank(7, w), ACT.Copy).then_inc(rdeg_ready, 1)

                def std(t, var, done):
                    sl = slice(blocks_of(t)[0], blocks_of(t)[-1] + 1)
                    act.wait_ge(var, t + 1)
                    a.activation(rstd[0:P, sl], rstd[0:P, sl], ACT.Sqrt, bias=eps_col[0:P, 0:1]).then_inc(done, 1)

                def scale(t):
                    act.wait_ge(gback_ready, t // 2 + 1)
                    if t >= 2:
                        act.wait_ge(gadded, t - 1)
                    act.wait_ge(rn_ready, 1 if t < NT - 1 else 2)
                    for i, b in enumerate(blocks_of(t)):
                        ins = a.activation(gout[t % 2][0:P, i, :], back_bank(t)[0:P, i * H:(i + 1) * H], ACT.Copy,
                                           scale=rnode[0:P, b:b + 1])
                    ins.then_inc(gscaled, 1)

                def last_std(k):
                    first, end = PARTS[k]
                    act.wait_ge(var_ready, k + 1 + (NT if gen else 0))
                    a.activation(rstd[0:P, first:end], rstd[0:P, first:end], ACT.Sqrt, bias=eps_col[0:P, 0:1]
                                 ).then_inc(std_ready, 1)

                if gen:
                    for t in range(NT):
                        std(t, var_ready, std_ready)
                        hand_over(0, t, gen)
                else:
                    act.wait_ge(esum_ready, ITS + 2)
                    scale(0)
                    scale(1)
                    std(0, gvar_ready, gstd_ready)
                    scale(2)
                    std(1, gvar_ready, gstd_ready)
                    for t in range(NT):
                        if t + 3 < NT:
                            scale(t + 3)
                        sl = slice(blocks_of(t)[0], blocks_of(t)[-1] + 1)
                        act.wait_ge(normed, t + 1)
                        a.activation(parts[0][0:P, sl, 0:H], X0[0:P, sl, :], ACT.Copy).then_inc(h_ready, 1)
                        if t == 0:
                            gcn_sums(ITS, 1)
                        if t + 2 < NT:
                            std(t + 2, gvar_ready, gstd_ready)
                        if t == 0:
                            gcn_out(ITS, 1)
                        if t >= 1:
                            hand_over(0, t - 1, gen)
                        if t == 5:
                            spread(0)
                    hand_over(0, NT - 1, gen)
                for r in range(2):
                    for t in range(NT):
                        S, G, n = NT * (r + gen) + t, NT * r + t, len(blocks_of(t))
                        gates = bank(2 + 2 * (S % 2), 512, P, 2).rearrange("p a (b f) -> p (a b) f", b=2)
                        if r == 0 and t + 1 < NT and not gen:
                            spread(t + 1)
                        act.wait_ge(gates_ready, S + 1)
                        if G > 0:
                            act.wait_ge(cand_used, G)
                        a.activation(rz[0:P, 0:n, :], gates[:, 0:n, 0:2 * H], ACT.Sigmoid).then_inc(rz_ready, 1)
                        act.wait_ge(gates_free, S + 1)
                        a.activation(cand[0:P, 0:n, :], cand[0:P, 0:n, :], ACT.Tanh).then_inc(tanh_ready, 1)
                        if r == 0:
                            hand_over(1, t, gen)
                        if r == 1 and t == 4:
                            last_std(0)
                last_std(1)
                last_std(2)

            def usual():
                act.activation(xparts[0:P, :, 0:H], X0[0:P, :, :], ACT.Copy).then_inc(xhigh_ready, 1)
                act.sem_inc(unit_free, 5)
                act.sem_inc(esum_free, 1)
                act.wait_ge(bias_done, 1)
                build_step(0, SU, SG, SS, False)
                with act.Fori(1, ITS) as it:
                    build_step(it, SU, SG, SS, True)
                build_step(ITS, LU, LG, LS, True)
                rounds(False)

            act.wait_ge(flag_ready, 1)
            bad_inputs = act.value_load(flag[0:1, 0:1], min_val=0, max_val=5)
            with act.If(bad_inputs == 0):
                usual()
            with act.Else():
                rounds(True)

        @block.tensor
        def _(pe):
            mm = nc.tensor.matmul

            pe.wait_ge(first_diag, 1)
            mm(bank(0, P, P), ones[0:P, 0:P], diag[0:P, 0:P], start=True, stop=True).then_inc(first_row, 1)
            pe.wait_ge(w_in, W_LOADS)
            for r in range(2):
                for k, c in enumerate((0, 2, 1, 1)):
                    ins = nc.tensor.transpose(bank(6 + r, 4 * H)[:, k * H:(k + 1) * H], wm_in[r][0:H, c, :],
                                              ident[0:H, 0:H])
                ins.then_inc(wt_ready, 1)
            pe.wait_ge(wt_copied, 2)
            nc.tensor.transpose(bank(6, H), w0_in[0:H, :], ident[0:H, 0:H]).then_inc(w0t_ready, 1)
            for r in range(2):
                if r:
                    pe.wait_ge(w_done, 1)
                rows = slice(32 * r, 32 * r + 3)
                rz_cols, n_cols = slice(0, 2 * H), slice(2 * H, 3 * H)
                mm(bank(4)[:, rz_cols], wmt[r][:, 0:2 * H], wi_in[r][:, rz_cols], start=True, stop=False)
                mm(bank(4)[:, rz_cols], ident[0:H, :], wh_in[r][0:H, rz_cols], start=False, stop=True)
                mm(bank(4)[:, n_cols], wmt[r][:, 0:2 * H], wi_in[r][:, n_cols], start=True, stop=True)
                mm(bank(7)[:, 0:3 * H], wmt[r][:, 2 * H:4 * H], wi_in[r], start=True, stop=True)
                for cols in (rz_cols, n_cols):
                    mm(bank(5)[rows, cols], bm3[r], wi_in[r][:, cols], start=True, stop=False)
                    mm(bank(5)[rows, cols], ones[0:1, 0:3], bi_in[r][0:1, cols], start=False, stop=cols == n_cols)
                    if cols == rz_cols:
                        mm(bank(5)[rows, cols], ones[0:1, 0:3], bh_in[r][0:1, cols], start=False, stop=True)
                mm(bank(5)[rows, 3 * H:4 * H], ones[0:1, 0:3], bh_in[r][0:1, 2 * H:3 * H], start=True, stop=True
                   ).then_inc(wp_ready, 1)
            pe.wait_ge(ptrs_ready, 3)
            mm(bank(3, NS, 1), ptr_f[0:P, 5:6], ident[0:P, 0:P], start=True, stop=True).then_inc(est_t, 1)
            pe.wait_ge(kwin_in, 5 * 16)
            for j in range(5):
                ins = nc.tensor.transpose(bank(j // 4)[:, (j % 4) * P:(j % 4) * P + P], kwin[0:P, j, :], ident[0:P, 0:P])
            ins.then_inc(win_t, 1)
            pe.wait_ge(ewin_ready, 1)
            for c in range(SC):
                ins = nc.tensor.transpose(bank(2)[:, c * NS:(c + 1) * NS],
                                          ewin_f[0:P, :].rearrange("p (e c) -> p e c", c=SC)[:, :, c], ident[0:P, 0:P])
            ins.then_inc(win_t, 1)
            pe.wait_ge(stats_ready, 1)
            mm(bank(3, 5, 1), ones[:, 0:1], stats, start=True, stop=True).then_inc(stats_sum, 1)

            def adjacency(it, i, ng):
                first, size = BATCHES[i]
                m = min(size, ng - first)
                if m <= 0:
                    return
                pe.wait_ge(one_ready, it * 12 + (2 * i + 2))
                for g in range(first, first + m):
                    u, k = g // 4, g % 4
                    if k == 0:
                        pe.wait_ge(unit_free, it * SU + (5 + (u - 4 if u > 4 else u - 2 if u < 3 else u - 7)))
                    ins = mm(bank(UBANK[u % 5])[:, k * P:k * P + P], one_lo[i % 3][:, g - first, :],
                             one_hi[i % 3][:, g - first, 0:P], start=True, stop=True)
                    if k == 3 or g == ng - 1:
                        ins.then_inc(unit_ready, 1)

            def edge_features(it, k):
                pe.wait_ge(onee_ready, it * 2 + (k // 5 + 1))
                for s in range(k, k + 5):
                    pe.wait_ge(e_in[s], it * 16 + 16)
                    for c in range(SC):
                        ins = mm(PS[H:128, 5, s * SD:(s + 1) * SD], ering[:, s, c, :], one_e[:, s, c, :],
                                 start=(c == 0), stop=(c == SC - 1))
                    ins.then_inc(e_used, 1)

            def gcn_sweep(i, w, first, last):
                for s in range(first, last):
                    ins = mm(bank(7, w), xparts[0:P, s, :], A3[0:P, s, bass.ds(i * STEP, w)],
                             start=(s == 0), stop=(s == NB - 1))
                if last == NB:
                    ins.then_inc(gsum_ready, 1)

            def gcn_dense(i, nb):
                pe.wait_ge(gsum_copied, i + 1)
                mm(bank(4, nb * P, H), w0t[:, :], gsum[:, 0:nb * P], start=True, stop=True).then_inc(gcn_ready, 1)

            def degrees(it, nb, prev):
                if prev:
                    pe.wait_ge(gcn_used, it)
                for b in range(nb):
                    for c in range(SC):
                        ins = mm(bank(4)[0:P, STEP + b:STEP + b + 1], one_eb[:, c, b * P:(b + 1) * P, 1],
                                 onesb[:, 0:1], start=(c == 0), stop=(c == SC - 1))
                ins.then_inc(esum_ready, 1)

            def build_step(it, ng, ns, prev):
                adjacency(it, 0, ng)
                adjacency(it, 1, ng)
                if prev:
                    pe.wait_ge(unit_free, it * SU + 5)
                    gcn_sweep(it - 1, STEP, 0, 13)
                adjacency(it, 2, ng)
                if prev:
                    gcn_sweep(it - 1, STEP, 13, NB)
                adjacency(it, 3, ng)
                pe.wait_ge(esum_free, it + 1)
                if ng == LG:
                    gcn_dense(it - 1, 2)
                edge_features(it, 0)
                if prev and ng > LG:
                    gcn_dense(it - 1, 2)
                adjacency(it, 4, ng)
                if ns > 5:
                    edge_features(it, 5)
                adjacency(it, 5, ng)
                degrees(it, ns // 5, prev)

            def sweep(S, t, first, last):
                w = len(blocks_of(t)) * P
                if first == 0 and S >= 2:
                    pe.wait_ge(agg_ready, S - 1)
                for s in range(first, last):
                    if t == 0 and s % 4 == 0:
                        pe.wait_ge(h_ready, S + s // 4 + 1)
                        pe.wait_ge(rest_used, S + s // 4 + 1)
                    ins = mm(bank(S % 2, w), parts[S // NT][0:P, s, :], A3[0:P, s, TILE * t:TILE * t + w],
                             start=(s == 0), stop=(s == NB - 1))
                if last == NB:
                    ins.then_inc(sweep_ready, 1)

            def gcn_back(tiles):
                for t in tiles:
                    for i, b in enumerate(blocks_of(t)):
                        ins = nc.tensor.transpose(back_bank(t)[0:P, i * H:(i + 1) * H], HE[0:H, b * P:(b + 1) * P],
                                                  ident[0:H, 0:H])
                ins.then_inc(gback_ready, 1)

            def spread(t):
                w = len(blocks_of(t)) * P
                pe.wait_ge(rdiag_ready, t + 1)
                if t:
                    pe.wait_ge(rdeg_ready, t)
                mm(bank(7, w), ones[0:P, :], rdiag[0:P, 0:w // P, :].rearrange("p b c -> p (b c)"),
                   start=True, stop=True).then_inc(spread_ready, 1)

            def dense(S, t, r, gen):
                if S >= 2:
                    pe.wait_ge(gates_free, S - 1)
                pe.wait_ge(agg_ready, S + 1)
                if r >= 0:
                    pe.wait_ge(he_ready, NT * r + t + 1)
                if r == 0 and not gen:
                    pe.wait_ge(emean_ready, t + 1)
                for i, b in enumerate(blocks_of(t)):
                    mean = agg[S % 2][:, i * P:(i + 1) * P]
                    own = HE[:, b * P:(b + 1) * P]
                    if r < 0:
                        ins = mm(PS[0:P, 2 + 2 * (S % 2), i * H:(i + 1) * H], mean, w0t[:, :], start=True, stop=True)
                        continue
                    at = 2 + 2 * (S % 2) + i // 2
                    lo = (i % 2) * 4 * H
                    mm(PS[0:P, at, lo:lo + 4 * H], own, w_he[r][:, :], start=True, stop=False)
                    mm(PS[0:P, at, lo:lo + 3 * H], mean, w_ag[r][:, :], start=False, stop=False)
                    if gen:
                        mm(PS[0:P, at, lo:lo + 4 * H], hneg[0:H + 1, b * P:(b + 1) * P], w_gen[r][0:H + 1, :],
                           start=False, stop=False)
                    ins = mm(PS[0:P, at, lo:lo + 4 * H], onesb[32 * r:32 * r + 3, 0:P], bias3[32 * r:32 * r + 3, :], start=False, stop=True)
                ins.then_inc(gates_ready, 1)

            def transposed(k, t):
                T, h = NT * k + t, (X0, H1)[k]
                pe.wait_ge(h_ready, T + 1)
                if T >= 1:
                    pe.wait_ge(he_ready, T)
                for i, b in enumerate(blocks_of(t)):
                    ins = nc.tensor.transpose(bank(6, 512, H)[:, i * P:(i + 1) * P], h[0:P, b, :], ident[0:P, 0:P])
                ins.then_inc(ht_ready, 1)

            def rounds(gen):
                if gen:
                    for rnd in range(3):
                        general_pass(2 + rnd)
                        for t in range(NT):
                            dense(NT * rnd + t, t, rnd - 1, gen)
                            if rnd < 2:
                                transposed(rnd, t)
                    return
                def two_sweeps(t):
                    for S in range(2):
                        sweep(S, S, 4 * t, min(4 * t + 4, NB))

                pe.wait_ge(gcn_used, ITS)
                for pair in ((0, 1), (2, 3), (4, 5)):
                    gcn_back(pair)
                gcn_sweep(ITS, P, 0, NB)
                for t in range(NT):
                    transposed(0, t)
                    if t == 0:
                        gcn_dense(ITS, 1)
                    if t >= 1:
                        two_sweeps(t - 1)
                    if t == 1:
                        pe.wait_ge(gcn_used, ITS + 1)
                        pe.wait_ge(gscaled, 2)
                        gcn_back((6,))
                    if t == 4:
                        spread(0)
                two_sweeps(NT - 1)
                for S in range(1, 2 * NT):
                    r, t = S // NT, S % NT
                    if S > 1:
                        sweep(S, t, 0, 10)
                    if 2 <= S < NT + 2:
                        transposed(1, S - 2)
                    if S < NT:
                        spread(S)
                    dense(S - 1, (S - 1) % NT, (S - 1) // NT, gen)
                    if S > 1:
                        sweep(S, t, 10, NB)
                dense(2 * NT - 1, NT - 1, 1, gen)

            def usual():
                pe.sem_inc(unit_ready, UCREDIT)
                pe.sem_inc(esum_ready, 1)
                build_step(0, SG, SS, False)
                pe.wait_ge(parts_ready, 1)
                with pe.Fori(1, ITS) as it:
                    build_step(it, SG, SS, True)
                build_step(ITS, LG, LS, True)
                pe.wait_ge(unit_free, 5 + SU * ITS + LU)
                pe.wait_ge(esum_free, ITS + 2)
                rounds(False)

            def general_pass(q):
                if q:
                    pe.wait_ge(sums_ready, q)
                if q > 2:
                    pe.wait_ge(he_ready, NT * (q - 2))
                    pe.wait_ge(gates_free, NT * (q - 2))
                    pe.wait_ge(neg_ready, 2 + q - 2)
                if q == 0:
                    pe.wait_ge(pass_zeroed, 2)
                tiles = [(t, len(blocks_of(t)) * P) for t in range(NT)]
                for t, w in tiles:
                    mm(bank(t, w), zero_st[0:P, :], iota_n[0:P, TILE * t:TILE * t + w], start=True, stop=False)
                with pe.Fori(0, EC) as c:
                    pe.wait_ge(gone_ready, c + (q * EC + 1))
                    if q == 1:
                        pe.wait_ge(estage_in, c * 16 + 16)
                    if q >= 2:
                        pe.wait_ge(stage_in, c * 16 + ((q - 2) * EC + 1) * 16)
                    for t, w in tiles:
                        ins = mm(bank(t, w), stage[0:P, :], one_n[0:P, TILE * t:TILE * t + w], start=False, stop=False)
                    ins.then_inc(gused, 1)
                for t, w in tiles:
                    ins = mm(bank(t, w), zero_st[0:P, :], iota_n[0:P, TILE * t:TILE * t + w], start=False, stop=True)
                ins.then_inc(pass_done, 1)

            def general():
                pe.wait_ge(bias_done, 1)
                pe.wait_ge(gen_c, 2)
                for r in range(2):
                    mm(bank(r, 3 * H, H + 1), wg_l[r], wi_in[r], start=True, stop=True).then_inc(gen_c, 1)
                pe.wait_ge(neg_ready, 2)
                pe.wait_ge(gz_ready, 1)
                pe.sem_inc(gused, 1)
                general_pass(0)
                general_pass(1)
                rounds(True)

            pe.wait_ge(w_done, 3)
            pe.wait_ge(flag_ready, 1)
            bad_inputs = pe.value_load(flag[0:1, 0:1], min_val=0, max_val=5)
            with pe.If(bad_inputs == 0):
                usual()
            with pe.Else():
                general()


_INS = ["x", "src", "dst", "edge_attr_64", "L0_gnn_W", "L1_gnn_W_msg", "L1_gnn_b_msg", "L1_gnn_W_ih", "L1_gnn_W_hh",
        "L1_gnn_b_ih", "L1_gnn_b_hh"]


def kernel(**inputs):
    import numpy as np
    import concourse.bacc as bacc
    from concourse.bass_utils import run_bass_kernel_spmd

    nc = bacc.Bacc("TRN2", target_bir_lowering=False, num_devices=1, dynamic_dma_scratch_size=4096)
    arrays, args = {}, []
    for name in _INS:
        a = np.ascontiguousarray(inputs[name])
        arrays[f"in_{name}"] = a
        args.append(nc.dram_tensor(f"in_{name}", a.shape, mybir.dt.from_np(a.dtype), kind="ExternalInput").ap())
    out = nc.dram_tensor("out_0", (N, H), mybir.dt.float32, kind="ExternalOutput").ap()
    build(nc, *args, out)
    r = run_bass_kernel_spmd(nc, [arrays], core_ids=[0])
    return r.results[0]["out_0"]
```
